# Optimizing a Trainium2 kernel written in Bass

```python
import numpy as np
import jax
import jax.numpy as jnp

def _softmax(x, axis=-1):
    return jax.nn.softmax(x, axis=axis)

def _gelu(x):
    return jax.nn.gelu(x, approximate=True)

def _silu(x):
    return jax.nn.silu(x)

def _sigmoid(x):
    return jax.nn.sigmoid(x)

def _layernorm(x, axis=-1, eps=1e-05):
    m = jnp.mean(x, axis=axis, keepdims=True)
    v = jnp.var(x, axis=axis, keepdims=True)
    return (x - m) / jnp.sqrt(v + eps)

def _scatter_add(tgt, idx, src, axis=0):
    return tgt.at[idx].add(src)

def _segment_sum(src, seg, n):
    return jax.ops.segment_sum(src, seg, n)
kernel_name = 'mk_adaln_attn_ffn_d1_seqx_r8_04c0f9'

def setup_inputs(seed: int=0):
    np.random.seed(seed)
    _w = jnp.asarray

    def _rec_inputs():
        import jax
        import jax.numpy as jnp
        _rk = jax.random.key(seed)
        x = -0.0003929 + 0.9999 * jax.random.normal(jax.random.fold_in(_rk, 1), (8, 128, 128), jnp.float32)
        _lenS = 128 - jax.random.randint(jax.random.fold_in(_rk, 7), (8,), 0, max(1, 128 // 4) + 1, jnp.int32)
        _lenS2 = 128 - jax.random.randint(jax.random.fold_in(_rk, 8), (8,), 0, max(1, 128 // 4) + 1, jnp.int32)
        itok_B_0_63 = jax.random.randint(jax.random.fold_in(_rk, 11), (8,), 0, 64, jnp.int32)
        condB_zX = jax.random.uniform(jax.random.fold_in(_rk, 12), (8,), jnp.float32, 0.0, 0.983423)
        condB_zY = jax.random.uniform(jax.random.fold_in(_rk, 13), (8,), jnp.float32, 0.0, 0.979075)
        condB_zR = jax.random.uniform(jax.random.fold_in(_rk, 14), (8,), jnp.float32, 0.0, 0.9968)
        return (x, itok_B_0_63, condB_zX, condB_zY, condB_zR)
    x, itok_B_0_63, condB_zX, condB_zY, condB_zR = _rec_inputs()

    def _L0_cond_setup():
        import jax, jax.numpy as jnp
        import numpy as np
        NUM_CATEGORIES = 64
        INPUT_DIM = 128
        HIDDEN_DIM = 128
        B = 32
        S = 64
        key = jax.random.key(seed)
        kx, kc, kw = jax.random.split(key, 3)
        x = jax.random.normal(kx, (B, S, INPUT_DIM), dtype=jnp.float32)
        cat_ids = jax.random.randint(kc, (B,), 0, NUM_CATEGORIES, dtype=jnp.int32)
        W = 0.02 * jax.random.normal(kw, (NUM_CATEGORIES, INPUT_DIM, HIDDEN_DIM), dtype=jnp.float32)
        b = jnp.zeros((NUM_CATEGORIES, HIDDEN_DIM), dtype=jnp.float32)
        return {'x': x, 'cat_ids': cat_ids, 'W': W, 'b': b}
    _L0_cond_all = _L0_cond_setup()
    _L0_cond_in = {k: v for k, v in _L0_cond_all.items() if k in ('W', 'b')}
    del _L0_cond_all

    def _L0_attn_setup():
        import jax, jax.numpy as jnp
        import numpy as np
        import math
        D_MODEL = 128
        N_HEADS = 16
        D_HEAD = D_MODEL // N_HEADS
        LSR_RANK = 32
        B, T = (4, 256)
        key = jax.random.key(seed)
        ks = jax.random.split(key, 11)
        s = 1.0 / math.sqrt(D_MODEL)
        x = jax.random.normal(ks[0], (B, T, D_MODEL), dtype=jnp.float32)
        Wq = jax.random.uniform(ks[1], (D_MODEL, D_MODEL), minval=-s, maxval=s)
        bq = jax.random.uniform(ks[2], (D_MODEL,), minval=-s, maxval=s)
        Wk = jax.random.uniform(ks[3], (D_MODEL, D_MODEL), minval=-s, maxval=s)
        bk = jax.random.uniform(ks[4], (D_MODEL,), minval=-s, maxval=s)
        Wv = jax.random.uniform(ks[5], (D_MODEL, D_MODEL), minval=-s, maxval=s)
        bv = jax.random.uniform(ks[6], (D_MODEL,), minval=-s, maxval=s)
        Wo = jax.random.uniform(ks[7], (D_MODEL, D_MODEL), minval=-s, maxval=s)
        bo = jax.random.uniform(ks[8], (D_MODEL,), minval=-s, maxval=s)
        Wq_lsr = jax.random.normal(ks[9], (N_HEADS, D_HEAD, LSR_RANK)) / math.sqrt(D_HEAD)
        Wk_lsr = jax.random.normal(ks[10], (N_HEADS, D_HEAD, LSR_RANK)) / math.sqrt(D_HEAD)
        return {'x': x, 'Wq': Wq, 'bq': bq, 'Wk': Wk, 'bk': bk, 'Wv': Wv, 'bv': bv, 'Wo': Wo, 'bo': bo, 'Wq_lsr': Wq_lsr, 'Wk_lsr': Wk_lsr}
    _L0_attn_all = _L0_attn_setup()
    _L0_attn_in = {k: v for k, v in _L0_attn_all.items() if k in ('Wq', 'bq', 'Wk', 'bk', 'Wv', 'bv', 'Wo', 'bo', 'Wq_lsr', 'Wk_lsr')}
    del _L0_attn_all

    def _L0_cond2_setup():
        import jax, jax.numpy as jnp
        import numpy as np
        key = jax.random.key(seed)
        k1, k2, k3, k4 = jax.random.split(key, 4)
        B, H, W = (64, 128, 128)
        return {'y': jax.random.uniform(k1, (B, H, W), dtype=jnp.float32), 'zX': jax.random.uniform(k2, (B, 1), dtype=jnp.float32), 'zY': jax.random.uniform(k3, (B, 1), dtype=jnp.float32), 'zR': jax.random.uniform(k4, (B, 1), dtype=jnp.float32), 'dx': 1, 'dy': 1}
    _L0_cond2_all = _L0_cond2_setup()
    _L0_cond2_in = {k: v for k, v in _L0_cond2_all.items() if k in ()}
    del _L0_cond2_all

    def _L0_ffn_setup():
        import jax, jax.numpy as jnp
        import numpy as np
        E = 8
        TOP_K = 2
        D = 128
        H = 2 * D
        key = jax.random.key(seed)
        k0, k1, k2, k3, k4 = jax.random.split(key, 5)
        scale = 0.02
        x = jax.random.normal(k0, (4, 256, D), dtype=jnp.float32)
        Wg = jax.random.normal(k1, (D, E), dtype=jnp.float32) * scale
        W1 = jax.random.normal(k2, (E, D, H), dtype=jnp.float32) * scale
        W2 = jax.random.normal(k3, (E, D, H), dtype=jnp.float32) * scale
        W3 = jax.random.normal(k4, (E, H, D), dtype=jnp.float32) * scale
        return {'x': x, 'Wg': Wg, 'W1': W1, 'W2': W2, 'W3': W3}
    _L0_ffn_all = _L0_ffn_setup()
    _L0_ffn_in = {k: v for k, v in _L0_ffn_all.items() if k in ('Wg', 'W1', 'W2', 'W3')}
    del _L0_ffn_all
    return {'x': x, 'itok_B_0_63': itok_B_0_63, 'condB_zX': condB_zX, 'condB_zY': condB_zY, 'condB_zR': condB_zR, 'L0_cond_W': _L0_cond_in['W'], 'L0_cond_b': _L0_cond_in['b'], 'L0_attn_Wq': _L0_attn_in['Wq'], 'L0_attn_bq': _L0_attn_in['bq'], 'L0_attn_Wk': _L0_attn_in['Wk'], 'L0_attn_bk': _L0_attn_in['bk'], 'L0_attn_Wv': _L0_attn_in['Wv'], 'L0_attn_bv': _L0_attn_in['bv'], 'L0_attn_Wo': _L0_attn_in['Wo'], 'L0_attn_bo': _L0_attn_in['bo'], 'L0_attn_Wq_lsr': _L0_attn_in['Wq_lsr'], 'L0_attn_Wk_lsr': _L0_attn_in['Wk_lsr'], 'L0_ffn_Wg': _L0_ffn_in['Wg'], 'L0_ffn_W1': _L0_ffn_in['W1'], 'L0_ffn_W2': _L0_ffn_in['W2'], 'L0_ffn_W3': _L0_ffn_in['W3']}

def reference(x, itok_B_0_63, condB_zX, condB_zY, condB_zR, L0_cond_W, L0_cond_b, L0_attn_Wq, L0_attn_bq, L0_attn_Wk, L0_attn_bk, L0_attn_Wv, L0_attn_bv, L0_attn_Wo, L0_attn_bo, L0_attn_Wq_lsr, L0_attn_Wk_lsr, L0_ffn_Wg, L0_ffn_W1, L0_ffn_W2, L0_ffn_W3):
    import jax
    import jax.numpy as jnp

    def _L0_cond_ref(x, cat_ids, W, b):
        import jax, jax.numpy as jnp
        import numpy as np
        NUM_CATEGORIES = 64
        INPUT_DIM = 128
        HIDDEN_DIM = 128
        B = 32
        S = 64
        selected_W = W[cat_ids]
        selected_b = b[cat_ids]
        out = jnp.einsum('bsd,bdh->bsh', x, selected_W) + selected_b[:, None, :]
        return out

    def _L0_attn_ref(x, Wq, bq, Wk, bk, Wv, bv, Wo, bo, Wq_lsr, Wk_lsr):
        import jax, jax.numpy as jnp
        import numpy as np
        import math
        D_MODEL = 128
        N_HEADS = 16
        D_HEAD = D_MODEL // N_HEADS
        LSR_RANK = 32
        B, T = (4, 256)
        Bq, Tq, _ = x.shape

        def split_heads(y):
            return y.reshape(Bq, Tq, N_HEADS, D_HEAD).transpose(0, 2, 1, 3)
        q = split_heads(x @ Wq.T + bq)
        k = split_heads(x @ Wk.T + bk)
        v = split_heads(x @ Wv.T + bv)
        q_lr = jnp.einsum('bhtd,hdr->bhtr', q, Wq_lsr)
        k_lr = jnp.einsum('bhtd,hdr->bhtr', k, Wk_lsr)
        scale = 1.0 / math.sqrt(max(LSR_RANK, 1))
        scores = jnp.einsum('bhir,bhjr->bhij', q_lr, k_lr) * scale
        causal_mask = jnp.triu(jnp.ones((Tq, Tq), dtype=bool), k=1)
        scores = jnp.where(causal_mask, jnp.float32(-jnp.inf), scores)
        attn = jax.nn.softmax(scores, axis=-1)
        y = jnp.einsum('bhij,bhjd->bhid', attn, v)
        y = y.transpose(0, 2, 1, 3).reshape(Bq, Tq, D_MODEL)
        return y @ Wo.T + bo

    def _L0_cond2_ref(y, zX, zY, zR, dx, dy):
        import jax, jax.numpy as jnp
        import numpy as np
        yp_x = jnp.pad(y, ((0, 0), (0, 0), (1, 1)), mode='reflect')
        lap_x = (yp_x[:, :, :-2] - 2.0 * y + yp_x[:, :, 2:]) / (dx * dx)
        yp_y = jnp.pad(y, ((0, 0), (1, 1), (0, 0)), mode='reflect')
        lap_y = (yp_y[:, :-2, :] - 2.0 * y + yp_y[:, 2:, :]) / (dy * dy)
        du_dt = zX[:, :, None] * lap_x + zY[:, :, None] * lap_y + zR[:, :, None] * y * (1.0 - y)
        return du_dt

    def _L0_ffn_ref(x, Wg, W1, W2, W3):
        import jax, jax.numpy as jnp
        import numpy as np
        E = 8
        TOP_K = 2
        D = 128
        H = 2 * D
        logits = jnp.einsum('bsd,de->bse', x, Wg)
        top_vals, top_idx = jax.lax.top_k(logits, TOP_K)
        probs = jax.nn.softmax(top_vals, axis=-1)
        onehot = jax.nn.one_hot(top_idx, E, dtype=x.dtype)
        weights = jnp.einsum('bsk,bske->bse', probs, onehot)
        out = jnp.zeros_like(x)
        for e in range(E):
            u = jnp.einsum('bsd,dh->bsh', x, W1[e])
            v = jnp.einsum('bsd,dh->bsh', x, W2[e])
            h = u * jax.nn.sigmoid(u) * v
            y = jnp.einsum('bsh,hd->bsd', h, W3[e])
            out = out + y * weights[..., e][..., None]
        return out
    x = x + _L0_attn_ref(_L0_cond_ref(x, itok_B_0_63, L0_cond_W, L0_cond_b), L0_attn_Wq, L0_attn_bq, L0_attn_Wk, L0_attn_bk, L0_attn_Wv, L0_attn_bv, L0_attn_Wo, L0_attn_bo, L0_attn_Wq_lsr, L0_attn_Wk_lsr)
    x = x + _L0_ffn_ref(_L0_cond2_ref(x, condB_zX[:, None], condB_zY[:, None], condB_zR[:, None], 1, 1), L0_ffn_Wg, L0_ffn_W1, L0_ffn_W2, L0_ffn_W3)
    return x

_drawn_inputs = setup_inputs


def setup_inputs(seed=0):
    import zlib

    import numpy as np

    out = dict(_drawn_inputs(seed))
    spreads = {'L0_cond_b': (0.0, 0.1)}
    factors = {'condB_zX': 2.922,
     'condB_zY': 4.148,
     'L0_cond_W': 3.619,
     'L0_attn_Wq': 8.0,
     'L0_attn_bq': 8.0,
     'L0_attn_Wk': 8.0,
     'L0_attn_bk': 8.0,
     'L0_attn_Wq_lsr': 8.0,
     'L0_attn_Wk_lsr': 8.0}
    for name, (base, spread) in spreads.items():
        noise = np.random.default_rng([zlib.crc32(name.encode()), seed]).standard_normal(out[name].shape)
        drawn = base * np.exp(spread * noise) if base else spread * noise
        out[name] = jnp.asarray(drawn.astype(out[name].dtype))
    for name, factor in factors.items():
        out[name] = (out[name] * factor).astype(out[name].dtype)
    return out
```

```python
import concourse.bass as bass
from concourse import mybir
from contextlib import ExitStack


def adaln_attention_reaction_moe(
    nc: bass.Bass,
    x: bass.AP,
    category: bass.AP,
    coef_x: bass.AP,
    coef_y: bass.AP,
    coef_r: bass.AP,
    cond_w: bass.AP,
    cond_b: bass.AP,
    wq: bass.AP,
    bq: bass.AP,
    wk: bass.AP,
    bk: bass.AP,
    wv: bass.AP,
    bv: bass.AP,
    wo: bass.AP,
    bo: bass.AP,
    wq_lsr: bass.AP,
    wk_lsr: bass.AP,
    w_gate: bass.AP,
    w1: bass.AP,
    w2: bass.AP,
    w3: bass.AP,
    out: bass.AP,
):
    F32 = mybir.dt.float32
    F32R = mybir.dt.float32r
    BF16 = mybir.dt.bfloat16
    I32 = mybir.dt.int32
    U32 = mybir.dt.uint32
    ALU = mybir.AluOpType
    ACT = mybir.ActivationFunctionType
    AX = mybir.AxisListType.X

    B, T, D = x.shape
    CATS = cond_w.shape[0]
    H, DH, RANK = wq_lsr.shape
    E, _, HID = w1.shape
    PAIRS = B // 2
    HALF = B // 2
    QR = 4
    QC = H // QR
    SLOTS = 2 * E
    GROUPS = 2 * QR
    SCALE = float(RANK) ** -0.5
    MASKED = -1e30
    assert D == T == H * DH == 128 and HID == 256 and B == 8 and QC == 4

    ctx = ExitStack()
    with ctx:
        def sb(name, shape, dt=F32):
            return ctx.enter_context(nc.sbuf_tensor(name, shape, dt))

        def pb(name):
            return ctx.enter_context(nc.psum_tensor(name, [128, 512], F32))

        def sem(name):
            return ctx.enter_context(nc.semaphore(name))

        x_nat = sb("x_nat", [T, B, D])
        cond_w_sb = sb("cond_w_sb", [D, B, D])
        cond_b_sb = sb("cond_b_sb", [CATS, D])
        proj_w = sb("proj_w", [128, 3, D])
        wk_nat = sb("wk_nat", [128, D])
        lsr_nat = sb("lsr_nat", [128, 2, RANK])
        cols_in = sb("cols_in", [128, 3])
        bo_rows = sb("bo_rows", [T, D])
        cat_row = sb("cat_row", [1, B], I32)
        cat_i = sb("cat_i", [CATS, B], I32)
        coef_rows = sb("coef_rows", [T, 3, B])
        w_gate_sb = sb("w_gate_sb", [D, E])
        w12_nat = sb("w12_nat", [D, 2, E, HID])
        w3_sb = sb("w3_sb", [128, E, 2, D])
        ident = sb("ident", [128, 128])
        ident_b = sb("ident_b", [128, 128], BF16)
        causal_b = sb("causal_b", [T, QC, T], BF16)
        head_rows = sb("head_rows", [128, H])
        stencil = sb("stencil", [T, T])
        part_i = sb("part_i", [CATS, 1], I32)
        part_f = sb("part_f", [CATS, 1])
        expert_i = sb("expert_i", [T, E], I32)
        expert_f = sb("expert_f", [T, E])
        proj_wT = sb("proj_wT", [D, 3, 128])
        lsrT = sb("lsrT", [RANK, 2, 128])
        fold = sb("fold", [128, 128])
        wkT = sb("wkT", [D, 128])
        bk_fold = sb("bk_fold", [128, 1])
        cat_f = sb("cat_f", [CATS, B])
        onehot = sb("onehot", [CATS, B])
        cond_bias = sb("cond_bias", [D, B])
        w12_hi = sb("w12_hi", [D, 2, E, HID], F32R)
        w12_lo = sb("w12_lo", [D, 2, E, HID], F32R)
        coef = sb("coef", [T, PAIRS, 4, 2])
        xT = sb("xT", [D, B, T])
        hT = sb("hT", [D, B, T])
        qk_all = sb("qk_all", [128, PAIRS, 2, 2 * T])
        v_all = sb("v_all", [T, PAIRS, 2, D])
        xbo_all = sb("xbo_all", [T, PAIRS, 2, D])
        qk = sb("qk", [128, 2, 2, T])
        k_head = sb("k_head", [128, 2, QR, QC, T])
        v_pad = sb("v_pad", [T, 2 * QC, 160])
        coef_p = sb("coef_p", [T, 4, 2])
        neg_max = sb("neg_max", [T, 2, QC])
        probs = sb("probs", [T, 2, QC, T])
        row_sum = sb("row_sum", [T, 2, QC, QR])
        inv_sum = sb("inv_sum", [T, 2 * H])
        probsT = sb("probsT", [T, 2, QC, T])
        yT_raw = sb("yT_raw", [128, 2, T])
        y_nat = sb("y_nat", [T, 2, D])
        yT = sb("yT", [128, 2, T])
        x1 = sb("x1", [T, 2, D + 2])
        side_sum = sb("side_sum", [T, 2, D])
        react = sb("react", [T, 2, D])
        react_x = sb("react_x", [T, 2, D])
        du_part = sb("du_part", [T, 2, D])
        du = sb("du", [T, 2, D])
        duT = sb("duT", [D, 2, T])
        duT_hi = sb("duT_hi", [D, 2 * T], F32R)
        duT_lo = sb("duT_lo", [D, 2 * T], F32R)
        logits = sb("logits", [T, 2, E])
        top8 = sb("top8", [T, 2, 8])
        top_i = sb("top_i", [T, 2, 8], U32)
        top_f = sb("top_f", [T, 2, 2])
        gap = sb("gap", [T, 2])
        gap_t = sb("gap_t", [T, 2])
        gate2 = sb("gate2", [T, 2, 2])
        pick = sb("pick", [T, 2, 2, E])
        gates = sb("gates", [T, 2, E])
        tanh_u = sb("tanh_u", [128, 2, 2 * T])
        silu_u = sb("silu_u", [128, 2, 2 * T])
        hidden = sb("hidden", [128, 2, 2, T])
        acc = sb("acc", [T, 2, D])
        result = sb("result", [T, 2, D])

        ps_uv = [pb("ps_uv0"), pb("ps_uv1")]
        ps_s = [pb("ps_s0"), pb("ps_s1")]
        ps_t = pb("ps_t")
        ps_y = [pb("ps_y0"), pb("ps_y1")]
        ps_m = pb("ps_m")

        in_x = [sem("in_x0"), sem("in_x1")]
        in_cat = sem("in_cat")
        in_cond_w = [sem(f"in_cond_w{b}") for b in range(B)]
        in_cond_b = sem("in_cond_b")
        in_proj = sem("in_proj")
        in_wk = sem("in_wk")
        in_lsr = sem("in_lsr")
        in_cols = sem("in_cols")
        in_rows = sem("in_rows")
        in_coef = sem("in_coef")
        in_gate = sem("in_gate")
        in_w12 = [sem("in_w1"), sem("in_w2")]
        in_w3 = sem("in_w3")
        c_id = sem("c_id")
        c_causal = sem("c_causal")
        c_heads = sem("c_heads")
        c_stencil = sem("c_stencil")
        c_iota = sem("c_iota")
        c_zero = sem("c_zero")
        proj_tr = sem("proj_tr")
        proj_cp = sem("proj_cp")
        lsr_tr = sem("lsr_tr")
        lsr_cp = sem("lsr_cp")
        fold_mm = sem("fold_mm")
        fold_cp = sem("fold_cp")
        wk_mm = sem("wk_mm")
        wk_cp = sem("wk_cp")
        cast_done = sem("cast_done")
        onehot_done = sem("onehot_done")
        cb_mm = sem("cb_mm")
        cb_cp = sem("cb_cp")
        coef_done = sem("coef_done")
        hi_done = sem("hi_done")
        lo_done = sem("lo_done")
        xbo_done = sem("xbo_done")
        xT_mm = sem("xT_mm")
        xT_cp = sem("xT_cp")
        hT_mm = sem("hT_mm")
        hT_cp = sem("hT_cp")
        q_mm = sem("q_mm")
        q_cp = sem("q_cp")
        k_mm = sem("k_mm")
        k_cp = sem("k_cp")
        v_mm = sem("v_mm")
        v_cp = sem("v_cp")
        qk_staged = sem("qk_staged")
        v_staged = sem("v_staged")
        k_masked = sem("k_masked")
        s_done = sem("s_done")
        max_done = sem("max_done")
        exp_done = sem("exp_done")
        pT_done = sem("pT_done")
        pT_cp = sem("pT_cp")
        av_done = sem("av_done")
        yraw_cp = sem("yraw_cp")
        inv_done = sem("inv_done")
        ytr_done = sem("ytr_done")
        ynorm_done = sem("ynorm_done")
        yT_mm = sem("yT_mm")
        yT_cp = sem("yT_cp")
        o_done = sem("o_done")
        x1_done = sem("x1_done")
        x1_edges = sem("x1_edges")
        lap_done = sem("lap_done")
        side_done = sem("side_done")
        coef_staged = sem("coef_staged")
        react_done = sem("react_done")
        rx_done = sem("rx_done")
        dup_done = sem("dup_done")
        du_done = sem("du_done")
        duT_mm = sem("duT_mm")
        duT_cp = sem("duT_cp")
        duh_cp = sem("duh_cp")
        dul_cp = sem("dul_cp")
        lg_mm = sem("lg_mm")
        top_done = sem("top_done")
        index_done = sem("index_done")
        index_f = sem("index_f")
        gate2_done = sem("gate2_done")
        picked = sem("picked")
        gates_done = sem("gates_done")
        gap_done = sem("gap_done")
        gap_tanh = sem("gap_tanh")
        uv_done = sem("uv_done")
        tanh_done = sem("tanh_done")
        silu_done = sem("silu_done")
        hid_done = sem("hid_done")
        y_done = sem("y_done")
        acc_done = sem("acc_done")
        out_done = sem("out_done")

        block = ctx.enter_context(nc.Block())

        @block.sync
        def _(sp):
            sp.dma_start(cat_row[:, :], category.rearrange("(a b) -> a b", a=1)).then_inc(in_cat, 16)
            sp.dma_start(x_nat[:, 0:HALF, :], x[0:HALF].rearrange("b t d -> t b d")).then_inc(in_x[0], 16)
            sp.wait_ge(in_cat, 16)
            for b in range(B):
                cat = sp.value_load(cat_row[0:1, b:b + 1], min_val=0, max_val=CATS - 1)
                sp.dma_start(cond_w_sb[:, b, :], cond_w[bass.ds(cat, 1), :, :].rearrange("a d h -> (a d) h"))\
                  .then_inc(in_cond_w[b], 16)
            sp.dma_start(x_nat[:, HALF:B, :], x[HALF:B].rearrange("b t d -> t b d")).then_inc(in_x[1], 16)
            for i, w in enumerate((w1, w2)):
                sp.dma_start(w12_nat[:, i, :, :], w.rearrange("e d h -> d e h")).then_inc(in_w12[i], 16)
            sp.dma_start(w3_sb[:, :, :, :], w3.rearrange("e (c h) d -> h e c d", c=2)).then_inc(in_w3, 16)
            with sp.Fori(0, PAIRS) as f:
                sp.wait_ge(acc_done, E * f + E)
                sp.dma_start(out[bass.ds(2 * f, 2)].rearrange("b t d -> t b d"), result[:, :, :])\
                  .then_inc(out_done, 16)
            sp.wait_ge(out_done, 16 * PAIRS + 1)

        @block.gpsimd
        def _(pool):
            pool.memset(ident[:, :], 0.0).then_inc(c_id, 1)
            pool.memset(causal_b[:, :, :], 0.0).then_inc(c_causal, 1)
            pool.memset(head_rows[:, :], 1.0).then_inc(c_heads, 1)
            pool.memset(stencil[:, :], 0.0).then_inc(c_stencil, 1)
            pool.iota(part_i[:, :], pattern=[[0, 1]], base=0, channel_multiplier=1).then_inc(c_iota, 1)
            pool.iota(expert_i[:, :], pattern=[[1, E]], base=0, channel_multiplier=0).then_inc(c_iota, 1)
            pool.wait_ge(c_id, 1)
            pool.affine_select(out=ident[:, :], in_=ident[:, :], compare_op=ALU.not_equal, fill=1.0,
                               base=0, pattern=[[-1, 128]], channel_multiplier=1).then_inc(c_id, 1)
            pool.wait_ge(c_heads, 1)
            pool.affine_select(out=head_rows[:, :], in_=head_rows[:, :], compare_op=ALU.is_ge, fill=0.0,
                               base=0, pattern=[[-DH, H]], channel_multiplier=1).then_inc(c_heads, 1)
            pool.wait_ge(c_heads, 2)
            pool.affine_select(out=head_rows[:, :], in_=head_rows[:, :], compare_op=ALU.is_ge, fill=0.0,
                               base=DH - 1, pattern=[[DH, H]], channel_multiplier=-1).then_inc(c_heads, 1)
            pool.wait_ge(c_causal, 1)
            pool.affine_select(out=causal_b[:, :, :], in_=causal_b[:, :, :], compare_op=ALU.is_ge, fill=MASKED,
                               base=0, pattern=[[0, QC], [-1, T]], channel_multiplier=1).then_inc(c_causal, 1)
            for n, (first, size, base, value) in enumerate(
                    [(0, T, 0, -2.0), (0, T, 1, 1.0), (0, T, -1, 1.0), (0, 1, -1, 2.0), (T - 1, 1, 2 - T, 2.0)]):
                pool.wait_ge(c_stencil, n + 1)
                cells = stencil[:, first:first + size]
                pool.affine_select(out=cells, in_=cells, compare_op=ALU.not_equal, fill=value,
                                   base=base, pattern=[[-1, size]], channel_multiplier=1).then_inc(c_stencil, 1)

            def mask_keys(rows):
                for r in rows:
                    for c in range(QC):
                        last = pool.tensor_scalar(k_head[:, :, r, c, :], qk[:, 1, :, :],
                                                  head_rows[:, QR * c + r:QR * c + r + 1], 1.0, ALU.mult, ALU.mult)
                    last.then_inc(k_masked, 1)

            def sides(p):
                pool.wait_ge(x1_edges, p + 1)
                pool.tensor_tensor(side_sum[:, :, :], x1[:, :, 0:D], x1[:, :, 2:D + 2], ALU.add)\
                    .then_inc(side_done, 1)

            pool.wait_ge(c_heads, 3)
            pool.wait_ge(qk_staged, 1)
            mask_keys(range(QR))
            pool.wait_ge(in_rows, 16)
            for half in range(2):
                pool.wait_ge(in_x[half], 16)
                for b in range(HALF * half, HALF * half + HALF):
                    last = pool.tensor_tensor(xbo_all[:, b // 2, b % 2, :], x_nat[:, b, :], bo_rows[:, :], ALU.add)
                last.then_inc(xbo_done, 1)
            for q in range(QC):
                pool.wait_ge(hi_done, q + 1)
                pool.tensor_tensor(w12_lo[:, 1, 2 * q:2 * q + 2, :], w12_nat[:, 1, 2 * q:2 * q + 2, :],
                                   w12_hi[:, 1, 2 * q:2 * q + 2, :].bitcast(F32), ALU.subtract).then_inc(lo_done, 1)
            sides(0)
            pool.wait_ge(qk_staged, 2)
            mask_keys(range(QR))
            with pool.Fori(0, PAIRS - 1) as f:
                sides(f + 1)
                mask_keys(range(QR))

        @block.scalar
        def _(act):
            for i, w in enumerate((wq, wv, wo)):
                act.dma_start(proj_w[:, i, :], w).then_inc(in_proj, 16)
            for i, w in enumerate((wq_lsr, wk_lsr)):
                act.dma_start(lsr_nat[:, i, :], w.rearrange("h d r -> (h d) r")).then_inc(in_lsr, 16)
            act.dma_start(wk_nat[:, :], wk).then_inc(in_wk, 16)
            act.dma_start(cat_i[:, :], category.rearrange("(a b) -> a b", a=1).to_broadcast([CATS, B]))\
               .then_inc(in_cond_b, 16)
            act.dma_start(cond_b_sb[:, :], cond_b).then_inc(in_cond_b, 16)
            for i, v in enumerate((bq, bk, bv)):
                act.dma_start(cols_in[:, i:i + 1], v.rearrange("(p a) -> p a", a=1)).then_inc(in_cols, 16)
            act.dma_start(bo_rows[:, :], bo.rearrange("(a d) -> a d", a=1).to_broadcast([T, D])).then_inc(in_rows, 16)
            for i, v in enumerate((coef_x, coef_y, coef_r)):
                act.dma_start(coef_rows[:, i, :], v.rearrange("(a b) -> a b", a=1).to_broadcast([T, B]))\
                   .then_inc(in_coef, 16)
            act.dma_start(w_gate_sb[:, :], w_gate).then_inc(in_gate, 16)

            def exps(p, g):
                G = GROUPS * p + g
                act.wait_ge(max_done, G + 1)
                if g >= 2 or not isinstance(p, int):
                    act.wait_ge(pT_done, G - 1)
                for c in range(QC):
                    last = nc.scalar.activation(probs[:, g % 2, c, :], ps_s[g % 2][:, T * c:T * c + T], ACT.Exp,
                                                bias=neg_max[:, g % 2, c:c + 1],
                                                accum_out=row_sum[:, g // QR, c, g % QR:g % QR + 1])
                last.then_inc(exp_done, 1)

            def copy_probsT(p, g):
                G = GROUPS * p + g
                act.wait_ge(pT_done, G + 1)
                if g >= 2 or not isinstance(p, int):
                    act.wait_ge(av_done, G - 1)
                nc.scalar.activation(probsT[:, g % 2, :, :], ps_t[:, :].rearrange("j (c i) -> j c i", c=QC), ACT.Copy)\
                    .then_inc(pT_cp, 1)

            def copy_yT(p):
                act.wait_ge(yT_mm, p + 1)
                nc.scalar.activation(yT[:, :, :], ps_m[:, 0:2 * T].rearrange("h (b i) -> h b i", b=2), ACT.Identity,
                                     bias=cols_in[:, 2:3]).then_inc(yT_cp, 1)

            def reaction(p):
                act.wait_ge(x1_done, p + 1)
                act.wait_ge(coef_staged, p + 1)
                for b in range(2):
                    last = nc.scalar.activation(react[:, b, :], x1[:, b, 1:D + 1], ACT.Identity,
                                                scale=coef_p[:, 2, b:b + 1], bias=coef_p[:, 3, b:b + 1])
                last.then_inc(react_done, 1)

            def copy_duT(p):
                act.wait_ge(duT_mm, p + 1)
                nc.scalar.activation(duT[:, :, :], ps_m[:, 0:2 * T].rearrange("d (b s) -> d b s", b=2), ACT.Copy)\
                    .then_inc(duT_cp, 1)

            def tanh_slot(f, s):
                act.wait_ge(uv_done, SLOTS * f + s + 1)
                nc.scalar.activation(tanh_u[:, s % 2, :], ps_uv[s % 2][:, 0:2 * T], ACT.Tanh, scale=0.5)\
                    .then_inc(tanh_done, 1)

            def tanh_gap(f):
                act.wait_ge(gap_done, f + 1)
                nc.scalar.activation(gap_t[:, :], gap[:, :], ACT.Tanh, scale=0.5).then_inc(gap_tanh, 1)

            def copy_xT(half):
                act.wait_ge(xT_mm, half + 1)
                nc.scalar.activation(xT[:, HALF * half:HALF * half + HALF, :],
                                     ps_uv[0][:, :].rearrange("d (b t) -> d b t", b=HALF), ACT.Copy).then_inc(xT_cp, 1)

            def copy_q(half):
                act.wait_ge(q_mm, half + 1)
                nc.scalar.activation(qk_all[:, 2 * half:2 * half + 2, 0, :],
                                     ps_y[0][:, :].rearrange("h (p t) -> h p t", p=2), ACT.Identity,
                                     bias=cols_in[:, 0:1]).then_inc(q_cp, 1)

            def copy_v(half):
                act.wait_ge(v_mm, half + 1)
                nc.scalar.activation(v_all[:, 2 * half:2 * half + 2, :, :],
                                     ps_uv[0][:, :].rearrange("t (p b h) -> t p b h", p=2, b=2), ACT.Copy)\
                    .then_inc(v_cp, 1)

            def round_w12(q):
                if q == 0:
                    act.wait_ge(in_w12[0], 16)
                    act.wait_ge(in_w12[1], 16)
                nc.scalar.activation(w12_hi[:, :, 2 * q:2 * q + 2, :], w12_nat[:, :, 2 * q:2 * q + 2, :], ACT.Copy)\
                    .then_inc(hi_done, 1)

            act.wait_ge(lsr_tr, 1)
            nc.scalar.activation(lsrT[:, :, :], ps_s[1][0:RANK, 0:256].rearrange("r (i h) -> r i h", i=2), ACT.Copy)\
                .then_inc(lsr_cp, 1)
            copy_xT(0)
            act.wait_ge(in_cols, 48)
            copy_q(0)
            copy_v(0)
            fill = {0: [lambda: copy_xT(1)], 2: [lambda: copy_q(1)], 3: [lambda: copy_v(1), lambda: round_w12(0)],
                    4: [lambda: round_w12(1)], 5: [lambda: round_w12(2)], 6: [lambda: round_w12(3)]}
            for g in range(GROUPS + 1):
                if g < GROUPS:
                    exps(0, g)
                if g >= 1:
                    copy_probsT(0, g - 1)
                for step in fill.get(g, []):
                    step()
            copy_yT(0)
            reaction(0)
            copy_duT(0)
            with act.Fori(0, PAIRS - 1) as f:
                for s in range(SLOTS):
                    tanh_slot(f, s)
                    if s < GROUPS:
                        exps(f + 1, s)
                    if 1 <= s <= GROUPS:
                        copy_probsT(f + 1, s - 1)
                    if s == 0:
                        tanh_gap(f)
                    if s == 11:
                        copy_yT(f + 1)
                    if s == 12:
                        reaction(f + 1)
                    if s == 14:
                        copy_duT(f + 1)
            for s in range(SLOTS):
                tanh_slot(PAIRS - 1, s)
                if s == 0:
                    tanh_gap(PAIRS - 1)

        @block.vector
        def _(dve):
            def row_max(p, g):
                dve.wait_ge(s_done, GROUPS * p + g + 1)
                nc.vector.tensor_reduce(neg_max[:, g % 2, :], ps_s[g % 2][:, :].rearrange("i (c j) -> i c j", c=QC),
                                        AX, ALU.max, negate=True).then_inc(max_done, 1)

            def stage_pair(p, gone):
                if gone is not None:
                    dve.wait_ge(s_done, GROUPS * gone)
                nc.vector.tensor_copy(qk[:, :, :, :], qk_all[:, bass.ds(p, 1), :, :]
                                      .rearrange("h p i (b t) -> h (p i) b t", b=2)).then_inc(qk_staged, 1)
                if gone is not None:
                    dve.wait_ge(av_done, GROUPS * gone)
                nc.vector.tensor_copy(
                    v_pad[:, :, :].rearrange("j n (r x) -> j n r x", r=QR)[:, :, :, 0:DH],
                    v_all[:, bass.ds(p, 1), :, :].rearrange("j p b (c r d) -> j (p b c) r d", c=QC, r=QR))\
                    .then_inc(v_staged, 1)

            def copy_yraw(p, b):
                dve.wait_ge(av_done, GROUPS * p + QR * (b + 1))
                nc.vector.tensor_copy(yT_raw[:, b, :], ps_m[:, T * b:T * b + T]).then_inc(yraw_cp, 1)

            def invert_sums(p):
                dve.wait_ge(exp_done, GROUPS * (p + 1))
                nc.vector.reciprocal(inv_sum[:, :], row_sum[:, :, :, :].rearrange("i b c r -> i (b c r)"))\
                    .then_inc(inv_done, 1)

            def norm_y(p):
                dve.wait_ge(ytr_done, p + 1)
                dve.wait_ge(inv_done, p + 1)
                nc.vector.tensor_tensor(
                    y_nat[:, :, :].rearrange("i b (h d) -> i (b h) d", h=H),
                    ps_m[:, 0:2 * D].rearrange("i (n d) -> i n d", d=DH),
                    inv_sum[:, :].rearrange("i (n a) -> i n a", a=1).to_broadcast([T, 2 * H, DH]),
                    ALU.mult).then_inc(ynorm_done, 1)

            def first_residual(p):
                dve.wait_ge(o_done, p + 1)
                nc.vector.tensor_tensor(x1[:, :, 1:D + 1], ps_m[:, 0:2 * D].rearrange("t (b d) -> t b d", b=2),
                                        xbo_all[:, bass.ds(p, 1), :, :].rearrange("t p b d -> t (p b) d"),
                                        ALU.add).then_inc(x1_done, 1)
                if not isinstance(p, int):
                    dve.wait_ge(react_done, p)
                nc.vector.tensor_copy(coef_p[:, :, :], coef[:, bass.ds(p, 1), :, :]
                                      .rearrange("t p k b -> t (p k) b")).then_inc(coef_staged, 1)
                dve.wait_ge(x1_done, p + 1)
                nc.vector.tensor_copy(x1[:, :, 0:D + 2:D + 1], x1[:, :, 2:D:D - 3]).then_inc(x1_edges, 1)

            def diffuse(p):
                dve.wait_ge(react_done, p + 1)
                nc.vector.tensor_tensor(react_x[:, :, :], react[:, :, :], x1[:, :, 1:D + 1], ALU.mult)\
                    .then_inc(rx_done, 1)
                dve.wait_ge(side_done, p + 1)
                dve.wait_ge(rx_done, p + 1)
                for b in range(2):
                    nc.vector.scalar_tensor_tensor(du_part[:, b, :], side_sum[:, b, :], coef_p[:, 0, b:b + 1],
                                                   react_x[:, b, :], ALU.mult, ALU.add).then_inc(dup_done, 1)
                dve.wait_ge(lap_done, p + 1)
                for b in range(2):
                    dve.wait_ge(dup_done, 2 * p + b + 1)
                    last = nc.vector.scalar_tensor_tensor(du[:, b, :], ps_m[:, D * b:D * b + D],
                                                          coef_p[:, 1, b:b + 1], du_part[:, b, :],
                                                          ALU.mult, ALU.add)
                last.then_inc(du_done, 1)

            def split_duT(p):
                if not isinstance(p, int):
                    dve.wait_ge(uv_done, SLOTS * p)
                dve.wait_ge(duT_cp, p + 1)
                flat = duT[:, :, :].rearrange("d b t -> d (b t)")
                nc.vector.tensor_copy(duT_hi[:, :], flat).then_inc(duh_cp, 1)
                dve.wait_ge(duh_cp, p + 1)
                nc.vector.tensor_tensor(duT_lo[:, :], flat, duT_hi[:, :].bitcast(F32), ALU.subtract)\
                    .then_inc(dul_cp, 1)

            def rank_experts(f):
                dve.wait_ge(lg_mm, f + 1)
                nc.vector.tensor_copy(logits[:, :, :], ps_m[:, 0:2 * E].rearrange("t (b e) -> t b e", b=2))
                for b in range(2):
                    last = nc.vector.max(top8[:, b, :], ps_m[:, E * b:E * b + E])
                last.then_inc(top_done, 1)
                dve.wait_ge(top_done, f + 1)
                nc.vector.tensor_tensor(gap[:, :].rearrange("t (b a) -> t b a", a=1), top8[:, :, 0:1],
                                        top8[:, :, 1:2], ALU.subtract).then_inc(gap_done, 1)
                for b in range(2):
                    last = nc.vector.max_index(top_i[:, b, :], top8[:, b, :], logits[:, b, :])
                last.then_inc(index_done, 1)
                dve.wait_ge(index_done, f + 1)
                nc.vector.tensor_copy(top_f[:, :, :], top_i[:, :, 0:2]).then_inc(index_f, 1)

            def weigh_experts(f):
                dve.wait_ge(gap_tanh, f + 1)
                for k, sign in enumerate((0.25, -0.25)):
                    nc.vector.tensor_scalar(gate2[:, :, k:k + 1], gap_t[:, :].rearrange("t (b a) -> t b a", a=1),
                                            sign, 0.25, ALU.mult, ALU.add).then_inc(gate2_done, 1)
                dve.wait_ge(index_f, f + 1)
                dve.wait_ge(gate2_done, 2 * f + 2)
                for b in range(2):
                    for k in range(2):
                        nc.vector.tensor_scalar(pick[:, k, b, :], expert_f[:, :], top_f[:, b, k:k + 1],
                                                gate2[:, b, k:k + 1], ALU.is_equal, ALU.mult).then_inc(picked, 1)
                dve.wait_ge(picked, 4 * f + 4)
                nc.vector.tensor_tensor(gates[:, :, :], pick[:, 0, :, :], pick[:, 1, :, :], ALU.add)\
                    .then_inc(gates_done, 1)

            def silu(f, s):
                dve.wait_ge(tanh_done, SLOTS * f + s + 1)
                nc.vector.scalar_tensor_tensor(silu_u[:, s % 2, :], tanh_u[:, s % 2, :], 1.0,
                                               ps_uv[s % 2][:, 0:2 * T], ALU.add, ALU.mult).then_inc(silu_done, 1)

            def gate_hidden(f, s):
                dve.wait_ge(silu_done, SLOTS * f + s + 1)
                nc.vector.tensor_tensor(hidden[:, s % 2, :, :].rearrange("h b t -> h (b t)"), silu_u[:, s % 2, :],
                                        ps_uv[s % 2][:, 2 * T:4 * T], ALU.mult).then_inc(hid_done, 1)

            def add_expert(f, e):
                dve.wait_ge(y_done, SLOTS * f + 2 * e + 2)
                if e == 0:
                    dve.wait_ge(gates_done, f + 1)
                else:
                    dve.wait_ge(acc_done, E * f + e)
                if e == E - 1:
                    dve.wait_ge(out_done, 16 * f + 1)
                for b in range(2):
                    base = x1[:, b, 1:D + 1] if e == 0 else acc[:, b, :]
                    into = result[:, b, :] if e == E - 1 else acc[:, b, :]
                    last = nc.vector.scalar_tensor_tensor(into, ps_y[e % 2][:, D * b:D * b + D],
                                                          gates[:, b, e:e + 1], base, ALU.mult, ALU.add)
                last.then_inc(acc_done, 1)

            def bias_h(half):
                dve.wait_ge(hT_mm, half + 1)
                part = slice(HALF * half, HALF * half + HALF)
                nc.vector.tensor_tensor(hT[:, part, :], ps_uv[1][:, :].rearrange("d (b t) -> d b t", b=HALF),
                                        cond_bias[:, part].rearrange("d (b a) -> d b a", a=1)
                                        .to_broadcast([D, HALF, T]), ALU.add).then_inc(hT_cp, 1)

            def bias_k(half):
                dve.wait_ge(k_mm, half + 1)
                nc.vector.tensor_scalar(qk_all[:, 2 * half:2 * half + 2, 1, :],
                                        ps_y[1][:, :].rearrange("h (p t) -> h p t", p=2), bk_fold[:, 0:1], None,
                                        ALU.add).then_inc(k_cp, 1)

            def w1_rest(q):
                dve.wait_ge(hi_done, q + 1)
                nc.vector.tensor_tensor(w12_lo[:, 0, 2 * q:2 * q + 2, :], w12_nat[:, 0, 2 * q:2 * q + 2, :],
                                        w12_hi[:, 0, 2 * q:2 * q + 2, :].bitcast(F32), ALU.subtract)\
                    .then_inc(lo_done, 1)

            nc.vector.memset(v_pad[:, :, :], 0.0).then_inc(c_zero, 1)
            nc.vector.memset(result[:, :, :], 0.0).then_inc(out_done, 1)
            dve.wait_ge(c_id, 2)
            nc.vector.tensor_copy(ident_b[:, :], ident[:, :]).then_inc(c_id, 1)
            dve.wait_ge(in_cond_b, 32)
            dve.wait_ge(c_iota, 2)
            nc.vector.tensor_copy(cat_f[:, :], cat_i[:, :]).then_inc(cast_done, 1)
            nc.vector.tensor_copy(part_f[:, :], part_i[:, :]).then_inc(cast_done, 1)
            nc.vector.tensor_copy(expert_f[:, :], expert_i[:, :]).then_inc(cast_done, 1)
            dve.wait_ge(cast_done, 3)
            nc.vector.tensor_scalar(onehot[:, :], cat_f[:, :], part_f[:, 0:1], None, ALU.is_equal)\
                .then_inc(onehot_done, 1)
            dve.wait_ge(proj_tr, 1)
            nc.vector.tensor_copy(proj_wT[:, :, :], ps_s[0][:, 0:384].rearrange("d (i h) -> d i h", i=3))\
                .then_inc(proj_cp, 1)
            dve.wait_ge(fold_mm, 1)
            dve.wait_ge(c_heads, 3)
            nc.vector.scalar_tensor_tensor(
                fold[:, :].rearrange("k (h d) -> k h d", h=H), ps_t[:, 0:128].rearrange("k (h d) -> k h d", h=H), SCALE,
                head_rows[:, :].rearrange("k (h a) -> k h a", a=1).to_broadcast([128, H, DH]), ALU.mult, ALU.mult)\
                .then_inc(fold_cp, 1)
            dve.wait_ge(cb_mm, 1)
            nc.vector.tensor_copy(cond_bias[:, :], ps_y[0][:, 0:B]).then_inc(cb_cp, 1)
            dve.wait_ge(cb_cp, 1)
            bias_h(0)
            dve.wait_ge(wk_mm, 1)
            nc.vector.tensor_copy(wkT[:, :], ps_y[1][:, 0:128]).then_inc(wk_cp, 1)
            nc.vector.tensor_copy(bk_fold[:, :], ps_y[1][:, 128:129]).then_inc(wk_cp, 1)
            dve.wait_ge(wk_cp, 2)
            bias_k(0)
            dve.wait_ge(k_cp, 1)
            dve.wait_ge(q_cp, 1)
            dve.wait_ge(v_cp, 1)
            dve.wait_ge(c_zero, 1)
            stage_pair(0, None)
            dve.wait_ge(in_coef, 48)

            def rows(i):
                return coef_rows[:, i, :].rearrange("t (p b) -> t p b", b=2)

            nc.vector.tensor_copy(coef[:, :, 0, :], rows(0)).then_inc(coef_done, 1)
            nc.vector.tensor_copy(coef[:, :, 1, :], rows(1)).then_inc(coef_done, 1)
            nc.vector.tensor_scalar(coef[:, :, 2, :], rows(2), -1.0, None, ALU.mult).then_inc(coef_done, 1)
            nc.vector.scalar_tensor_tensor(coef[:, :, 3, :], rows(0), -2.0, rows(2), ALU.mult, ALU.add)\
                .then_inc(coef_done, 1)
            fill = {1: [lambda: bias_h(1)], 3: [lambda: bias_k(1), lambda: copy_yraw(0, 0)],
                    4: [lambda: w1_rest(0)], 5: [lambda: w1_rest(1), lambda: copy_yraw(0, 0)],
                    6: [lambda: w1_rest(2)], 7: [lambda: w1_rest(3)]}
            fill[3] = fill[3][:1]
            for g in range(GROUPS):
                row_max(0, g)
                for step in fill.get(g, []):
                    step()
            copy_yraw(0, 1)
            invert_sums(0)
            norm_y(0)
            dve.wait_ge(k_cp, 2)
            dve.wait_ge(q_cp, 2)
            dve.wait_ge(v_cp, 2)
            stage_pair(1, 1)
            dve.wait_ge(xbo_done, 2)
            dve.wait_ge(coef_done, 4)
            first_residual(0)
            diffuse(0)
            split_duT(0)
            with dve.Fori(0, PAIRS - 1) as f:
                for s in range(SLOTS):
                    silu(f, s)
                    if s < GROUPS:
                        row_max(f + 1, s)
                    gate_hidden(f, s)
                    if s == 0:
                        rank_experts(f)
                    if s == 1:
                        weigh_experts(f)
                    if s >= 2 and s % 2 == 0:
                        add_expert(f, s // 2 - 1)
                    if s == 5:
                        copy_yraw(f + 1, 0)
                    if s == 9:
                        copy_yraw(f + 1, 1)
                        invert_sums(f + 1)
                    if s == 10:
                        norm_y(f + 1)
                        stage_pair((f + 2) % PAIRS, f + 2)
                    if s == 12:
                        first_residual(f + 1)
                    if s == 13:
                        diffuse(f + 1)
                    if s == 15:
                        split_duT(f + 1)
                add_expert(f, E - 1)
            for s in range(SLOTS):
                silu(PAIRS - 1, s)
                gate_hidden(PAIRS - 1, s)
                if s == 0:
                    rank_experts(PAIRS - 1)
                if s == 1:
                    weigh_experts(PAIRS - 1)
                if s >= 2 and s % 2 == 0:
                    add_expert(PAIRS - 1, s // 2 - 1)
            add_expert(PAIRS - 1, E - 1)

        @block.tensor
        def _(pe):
            mm = nc.tensor.matmul

            def transpose_x(half):
                pe.wait_ge(in_x[half], 16)
                if half:
                    pe.wait_ge(v_cp, half)
                for b in range(HALF):
                    last = nc.tensor.transpose(ps_uv[0][:, T * b:T * b + T], x_nat[:, HALF * half + b, :], ident[:, :])
                last.then_inc(xT_mm, 1)

            def condition(half):
                pe.wait_ge(xT_cp, half + 1)
                if half:
                    pe.wait_ge(hT_cp, half)
                for b in range(HALF):
                    pe.wait_ge(in_cond_w[HALF * half + b], 16)
                    last = mm(ps_uv[1][:, T * b:T * b + T], cond_w_sb[:, HALF * half + b, :],
                              xT[:, HALF * half + b, :], start=True, stop=True)
                last.then_inc(hT_mm, 1)

            def project_q(half):
                pe.wait_ge(hT_cp, half + 1)
                if half:
                    pe.wait_ge(q_cp, half)
                mm(ps_y[0][:, :], proj_wT[:, 0, :], hT[:, HALF * half:HALF * half + HALF, :],
                   start=True, stop=True).then_inc(q_mm, 1)

            def project_k(half):
                if half:
                    pe.wait_ge(k_cp, half)
                mm(ps_y[1][:, :], wkT[:, :], hT[:, HALF * half:HALF * half + HALF, :],
                   start=True, stop=True).then_inc(k_mm, 1)

            def project_v(half):
                pe.wait_ge(xT_cp, half + 1)
                for b in range(HALF):
                    last = mm(ps_uv[0][:, D * b:D * b + D], hT[:, HALF * half + b, :], proj_wT[:, 1, :],
                              start=True, stop=True)
                last.then_inc(v_mm, 1)

            def scores(p, g):
                G = GROUPS * p + g
                b, r = g // QR, g % QR
                pe.wait_ge(k_masked, QR * p + r + 1)
                if g >= 2 or not isinstance(p, int):
                    pe.wait_ge(exp_done, G - 1)
                mm(ps_s[g % 2][:, :], ident_b[:, :], causal_b[:, :, :], start=True, stop=False)
                mm(ps_s[g % 2][:, :], qk[:, 0, b, :], k_head[:, b, r, :, :], start=False, stop=True)\
                    .then_inc(s_done, 1)

            def transpose_probs(p, g):
                G = GROUPS * p + g
                pe.wait_ge(exp_done, G + 1)
                if g >= 1 or not isinstance(p, int):
                    pe.wait_ge(pT_cp, G)
                for c in range(QC):
                    last = nc.tensor.transpose(ps_t[:, T * c:T * c + T], probs[:, g % 2, c, :], ident[:, :])
                last.then_inc(pT_done, 1)

            def weigh_values(p, g):
                b, r = g // QR, g % QR
                pe.wait_ge(pT_cp, GROUPS * p + g + 1)
                if g == 0:
                    pe.wait_ge(v_staged, p + 1)
                    if not isinstance(p, int):
                        pe.wait_ge(top_done, p)
                if g == QR:
                    pe.wait_ge(yraw_cp, 2 * p + 1)
                for c in range(QC):
                    last = mm(ps_m[32 * c:32 * c + 32, T * b:T * b + T], v_pad[:, QC * b + c, 32 * r:32 * r + 32],
                              probsT[:, g % 2, c, :], start=r == 0, stop=r == QR - 1)
                last.then_inc(av_done, 1)

            def transpose_y(p):
                pe.wait_ge(yraw_cp, 2 * p + 2)
                for b in range(2):
                    last = nc.tensor.transpose(ps_m[:, D * b:D * b + D], yT_raw[:, b, :], ident[:, :])
                last.then_inc(ytr_done, 1)

            def transpose_y_back(p):
                pe.wait_ge(ynorm_done, p + 1)
                for b in range(2):
                    last = nc.tensor.transpose(ps_m[:, T * b:T * b + T], y_nat[:, b, :], ident[:, :])
                last.then_inc(yT_mm, 1)

            def project_out(p):
                pe.wait_ge(yT_cp, p + 1)
                for b in range(2):
                    last = mm(ps_m[:, D * b:D * b + D], yT[:, b, :], proj_wT[:, 2, :], start=True, stop=True)
                last.then_inc(o_done, 1)

            def laplace_tokens(p):
                pe.wait_ge(x1_done, p + 1)
                mm(ps_m[:, 0:2 * D], stencil[:, :], x1[:, :, 1:D + 1], start=True, stop=True).then_inc(lap_done, 1)

            def transpose_du(p):
                pe.wait_ge(du_done, p + 1)
                for b in range(2):
                    last = nc.tensor.transpose(ps_m[:, T * b:T * b + T], du[:, b, :], ident[:, :])
                last.then_inc(duT_mm, 1)

            def score_experts(p):
                pe.wait_ge(duT_cp, p + 1)
                for b in range(2):
                    last = mm(ps_m[:, E * b:E * b + E], duT[:, b, :], w_gate_sb[:, :], start=True, stop=True)
                last.then_inc(lg_mm, 1)

            def expert_up(f, s):
                e, c = s // 2, s % 2
                if s == 0:
                    pe.wait_ge(dul_cp, f + 1)
                if s >= 2:
                    pe.wait_ge(hid_done, SLOTS * f + s - 1)
                for i in range(2):
                    w_hi = w12_hi[:, i, e, 128 * c:128 * c + 128]
                    w_lo = w12_lo[:, i, e, 128 * c:128 * c + 128]
                    into = ps_uv[s % 2][:, 2 * T * i:2 * T * i + 2 * T]
                    mm(into, w_hi, duT_hi[:, :], start=True, stop=False)
                    mm(into, w_hi, duT_lo[:, :], start=False, stop=False)
                    last = mm(into, w_lo, duT_hi[:, :], start=False, stop=True)
                last.then_inc(uv_done, 1)

            def expert_down(f, s):
                e, c = s // 2, s % 2
                pe.wait_ge(hid_done, SLOTS * f + s + 1)
                if c == 0 and e >= 2:
                    pe.wait_ge(acc_done, E * f + e - 1)
                for b in range(2):
                    last = mm(ps_y[e % 2][:, D * b:D * b + D], hidden[:, s % 2, b, :], w3_sb[:, e, c, :],
                              start=c == 0 and b == 0, stop=c == 1, skip_group_check=True)
                last.then_inc(y_done, 1)

            pe.wait_ge(c_id, 2)
            pe.wait_ge(in_proj, 48)
            for i in range(3):
                last = nc.tensor.transpose(ps_s[0][:, 128 * i:128 * i + 128], proj_w[:, i, :], ident[:, :])
            last.then_inc(proj_tr, 1)
            pe.wait_ge(in_lsr, 32)
            for i in range(2):
                last = nc.tensor.transpose(ps_s[1][0:RANK, 128 * i:128 * i + 128], lsr_nat[:, i, :], ident[:, :])
            last.then_inc(lsr_tr, 1)
            transpose_x(0)
            pe.wait_ge(lsr_cp, 1)
            mm(ps_t[:, 0:128], lsrT[:, 1, :], lsrT[:, 0, :], start=True, stop=True).then_inc(fold_mm, 1)
            pe.wait_ge(onehot_done, 1)
            mm(ps_y[0][:, 0:B], cond_b_sb[:, :], onehot[:, :], start=True, stop=True).then_inc(cb_mm, 1)
            condition(0)
            pe.wait_ge(fold_cp, 1)
            pe.wait_ge(in_wk, 16)
            pe.wait_ge(in_cols, 48)
            mm(ps_y[1][:, 0:128], wk_nat[:, :], fold[:, :], start=True, stop=True)
            mm(ps_y[1][:, 128:129], fold[:, :], cols_in[:, 1:2], start=True, stop=True).then_inc(wk_mm, 1)
            pe.wait_ge(proj_cp, 1)
            pe.wait_ge(cb_cp, 1)
            project_q(0)
            pe.wait_ge(wk_cp, 2)
            project_k(0)
            project_v(0)
            pe.wait_ge(c_id, 3)
            pe.wait_ge(c_causal, 2)
            fill = {0: transpose_x, 1: condition, 2: project_q, 3: lambda half: (project_k(half), project_v(half))}
            for g in range(GROUPS + 2):
                if g < GROUPS:
                    scores(0, g)
                if 1 <= g <= GROUPS:
                    transpose_probs(0, g - 1)
                if g >= 2:
                    weigh_values(0, g - 2)
                if g in fill:
                    fill[g](1)
            transpose_y(0)
            transpose_y_back(0)
            project_out(0)
            pe.wait_ge(c_stencil, 6)
            laplace_tokens(0)
            transpose_du(0)
            pe.wait_ge(in_gate, 16)
            score_experts(0)
            pe.wait_ge(lo_done, 2 * QC)
            pe.wait_ge(in_w3, 16)
            with pe.Fori(0, PAIRS - 1) as f:
                for s in range(SLOTS):
                    expert_up(f, s)
                    if s < GROUPS:
                        scores(f + 1, s)
                    if s == SLOTS - 1:
                        score_experts(f + 1)
                    if s >= 1:
                        expert_down(f, s - 1)
                    if 1 <= s <= GROUPS:
                        transpose_probs(f + 1, s - 1)
                    if 2 <= s <= GROUPS + 1:
                        weigh_values(f + 1, s - 2)
                    if s == 10:
                        transpose_y(f + 1)
                    if s == 11:
                        transpose_y_back(f + 1)
                    if s == 12:
                        project_out(f + 1)
                    if s == 13:
                        laplace_tokens(f + 1)
                    if s == 14:
                        transpose_du(f + 1)
                expert_down(f, SLOTS - 1)
            for s in range(SLOTS):
                expert_up(PAIRS - 1, s)
                if s >= 1:
                    expert_down(PAIRS - 1, s - 1)
            expert_down(PAIRS - 1, SLOTS - 1)


_INS = ["x", "itok_B_0_63", "condB_zX", "condB_zY", "condB_zR", "L0_cond_W", "L0_cond_b", "L0_attn_Wq", "L0_attn_bq",
        "L0_attn_Wk", "L0_attn_bk", "L0_attn_Wv", "L0_attn_bv", "L0_attn_Wo", "L0_attn_bo", "L0_attn_Wq_lsr",
        "L0_attn_Wk_lsr", "L0_ffn_Wg", "L0_ffn_W1", "L0_ffn_W2", "L0_ffn_W3"]
_OUT = ((8, 128, 128), "float32")


def kernel(**inputs):
    import numpy as _np
    import concourse.bacc as _bacc
    from concourse import mybir as _mybir
    from concourse.bass_utils import run_bass_kernel_spmd as _run

    nc = _bacc.Bacc("TRN2", target_bir_lowering=False, num_devices=1)
    arrays, args = {}, []
    for name in _INS:
        a = _np.ascontiguousarray(inputs[name])
        arrays[f"in_{name}_dram"] = a
        args.append(nc.dram_tensor(f"in_{name}_dram", a.shape, _mybir.dt.from_np(a.dtype), kind="ExternalInput").ap())
    shape, dtype = _OUT
    args.append(nc.dram_tensor("out_dram", shape, _mybir.dt.from_np(_np.dtype(dtype)), kind="ExternalOutput").ap())
    adaln_attention_reaction_moe(nc, *args)
    r = _run(nc, [arrays], core_ids=[0])
    return r.results[0]["out_dram"]
```

```python
import concourse.bass as bass
from concourse import mybir
from contextlib import ExitStack


def adaln_attention_reaction_moe(
    nc: bass.Bass,
    x: bass.AP,
    category: bass.AP,
    coef_x: bass.AP,
    coef_y: bass.AP,
    coef_r: bass.AP,
    cond_w: bass.AP,
    cond_b: bass.AP,
    wq: bass.AP,
    bq: bass.AP,
    wk: bass.AP,
    bk: bass.AP,
    wv: bass.AP,
    bv: bass.AP,
    wo: bass.AP,
    bo: bass.AP,
    wq_lsr: bass.AP,
    wk_lsr: bass.AP,
    w_gate: bass.AP,
    w1: bass.AP,
    w2: bass.AP,
    w3: bass.AP,
    out: bass.AP,
):
    F32 = mybir.dt.float32
    F32R = mybir.dt.float32r
    BF16 = mybir.dt.bfloat16
    I32 = mybir.dt.int32
    U32 = mybir.dt.uint32
    ALU = mybir.AluOpType
    ACT = mybir.ActivationFunctionType
    AX = mybir.AxisListType.X

    B, T, D = x.shape
    CATS = cond_w.shape[0]
    H, DH, RANK = wq_lsr.shape
    E, _, HID = w1.shape
    PAIRS = B // 2
    HALF = B // 2
    QR = 4
    QC = H // QR
    SLOTS = 2 * E
    GROUPS = 2 * QR
    PARTS = 3
    STACK = PARTS * PARTS * DH
    SCALE = float(RANK) ** -0.5
    MASKED = -1e30
    assert D == T == H * DH == 128 and HID == 256 and B == 8 and QC == 4

    ctx = ExitStack()
    with ctx:
        def sb(name, shape, dt=F32):
            return ctx.enter_context(nc.sbuf_tensor(name, shape, dt))

        def pb(name):
            return ctx.enter_context(nc.psum_tensor(name, [128, 512], F32))

        def sem(name):
            return ctx.enter_context(nc.semaphore(name))

        def stack_of(p, i):
            return stack[:, i, :, :] if p == 1 else stack_kept[:, p - 2, i, :, :]

        def group_at(f, s, ahead):
            n = (s + 9) // 2
            if s % 2 == 0 or (n >= GROUPS and not ahead):
                return None
            return (f + 1, n) if n < GROUPS else (f + 2, n - GROUPS)

        def tail_bank(s):
            return ps_s[(s // 2 + s % 2 + 1) % 2][:, 0:2 * T]

        def later(p):
            return not isinstance(p, int) or p > 0

        x_nat = sb("x_nat", [T, B, D])
        cond_w_sb = sb("cond_w_sb", [D, B, D])
        cond_b_sb = sb("cond_b_sb", [CATS, D])
        proj_w = sb("proj_w", [128, 3, D])
        wk_nat = sb("wk_nat", [128, D])
        lsr_nat = sb("lsr_nat", [128, 2, RANK])
        cols_in = sb("cols_in", [128, 3])
        bo_rows = sb("bo_rows", [T, D])
        cat_row = sb("cat_row", [1, B], I32)
        cat_i = sb("cat_i", [CATS, B], I32)
        coef_rows = sb("coef_rows", [T, 3, B])
        w_gate_sb = sb("w_gate_sb", [D, E])
        w12_nat = sb("w12_nat", [D, 2, E, HID])
        w3_sb = sb("w3_sb", [128, E, 2, D])
        ident = sb("ident", [128, 128])
        ident_b = sb("ident_b", [128, 128], BF16)
        causal_b = sb("causal_b", [T, QC, T], BF16)
        head_rows = sb("head_rows", [128, H])
        stencil = sb("stencil", [T, T])
        part_i = sb("part_i", [CATS, 1], I32)
        part_f = sb("part_f", [CATS, 1])
        expert_i = sb("expert_i", [T, 4, E], I32)
        expert_f = sb("expert_f", [T, 4, E])
        proj_wT = sb("proj_wT", [D, 3, 128])
        lsrT = sb("lsrT", [RANK, 2, 128])
        fold = sb("fold", [128, 128])
        wkT = sb("wkT", [D, 128])
        bk_fold = sb("bk_fold", [128, 1])
        cat_f = sb("cat_f", [CATS, B])
        onehot = sb("onehot", [CATS, B])
        cond_bias = sb("cond_bias", [D, B])
        w12_hi = sb("w12_hi", [D, 2, E, HID], F32R)
        w12_lo = sb("w12_lo", [D, 2, E, HID], F32R)
        coef = sb("coef", [T, PAIRS, 4, 2])
        xT = sb("xT", [D, HALF, T])
        hT = sb("hT", [D, B, T])
        qk_all = sb("qk_all", [128, PAIRS, 2, 2 * T])
        qk_parts = sb("qk_parts", [128, PAIRS, PARTS, 2, 2 * T], BF16)
        qk_rest = sb("qk_rest", [128, 2, 2 * T])
        k_head = sb("k_head", [128, 2, QR, QC, T])
        stack_kept = sb("stack_kept", [STACK, PAIRS - 2, 2, H, 2 * T], BF16)
        v_all = sb("v_all", [T, PAIRS, 2, D])
        xbo_all = sb("xbo_all", [T, PAIRS, 2, D])
        stack = sb("stack", [STACK, 2, H, 2 * T], BF16)
        v_pad = sb("v_pad", [T, 2 * QC, 160])
        coef_p = sb("coef_p", [T, 4, 2])
        neg_max = sb("neg_max", [T, 2, QC])
        probs = sb("probs", [T, 2, QC, T])
        row_sum = sb("row_sum", [T, 2, QC, QR])
        inv_sum = sb("inv_sum", [T, 2 * H])
        probsT = sb("probsT", [T, 2, QC, T])
        yT_raw = sb("yT_raw", [128, 2, T])
        y_nat = sb("y_nat", [T, 2, D])
        yT = sb("yT", [128, 2, T])
        x1 = sb("x1", [T, 2, D + 2])
        side_sum = sb("side_sum", [T, 2, D])
        react = sb("react", [T, 2, D])
        react_x = sb("react_x", [T, 2, D])
        du_part = sb("du_part", [T, 2, D])
        du = sb("du", [T, 2, D])
        duT = sb("duT", [D, 2, T])
        duT_hi = sb("duT_hi", [D, 2 * T], F32R)
        duT_lo = sb("duT_lo", [D, 2 * T], F32R)
        logits = sb("logits", [T, 2, E])
        top8 = sb("top8", [T, 2, 8])
        top_i = sb("top_i", [T, 2, 8], U32)
        top_f = sb("top_f", [T, 2, 2])
        gap = sb("gap", [T, 2])
        gap_t = sb("gap_t", [T, 2])
        gate2 = sb("gate2", [T, 2, 2])
        same = sb("same", [T, 4, E])
        pick = sb("pick", [T, 2, 2, E])
        gates = sb("gates", [T, 2, E])
        tanh_u = sb("tanh_u", [128, 2, 2 * T])
        silu_u = sb("silu_u", [128, 2, 2 * T])
        hidden = sb("hidden", [128, 2, 2, T])
        acc = sb("acc", [T, 2, D])
        result = sb("result", [T, 2, D])

        q_trip = nc.dram_tensor("q_trip", [PAIRS, PARTS, DH, H, 2 * T], BF16).ap()
        k_trip = nc.dram_tensor("k_trip", [PAIRS, 2 * PARTS - 1, DH, H, 2 * T], BF16).ap()

        ps_uv = [pb("ps_uv0"), pb("ps_uv1")]
        ps_s = [pb("ps_s0"), pb("ps_s1")]
        ps_t = pb("ps_t")
        ps_y = [pb("ps_y0"), pb("ps_y1")]
        ps_m = pb("ps_m")

        in_x = [sem("in_x0"), sem("in_x1")]
        in_cat = sem("in_cat")
        in_cond_w = [sem(f"in_cond_w{b}") for b in range(B)]
        in_cond_b = sem("in_cond_b")
        in_proj = sem("in_proj")
        in_wo = sem("in_wo")
        in_wk = sem("in_wk")
        in_lsr = sem("in_lsr")
        in_cols = sem("in_cols")
        in_rows = sem("in_rows")
        in_coef = sem("in_coef")
        in_gate = sem("in_gate")
        in_w12 = [sem("in_w1"), sem("in_w2")]
        in_w3 = sem("in_w3")
        c_id = sem("c_id")
        c_causal = sem("c_causal")
        c_heads = sem("c_heads")
        c_stencil = sem("c_stencil")
        c_iota = sem("c_iota")
        c_zero = sem("c_zero")
        proj_tr = sem("proj_tr")
        proj_cp = sem("proj_cp")
        wo_tr = sem("wo_tr")
        wo_cp = sem("wo_cp")
        lsr_tr = sem("lsr_tr")
        lsr_cp = sem("lsr_cp")
        fold_mm = sem("fold_mm")
        fold_cp = sem("fold_cp")
        wk_mm = sem("wk_mm")
        wk_cp = sem("wk_cp")
        cast_done = sem("cast_done")
        onehot_done = sem("onehot_done")
        cb_mm = sem("cb_mm")
        cb_cp = sem("cb_cp")
        coef_done = sem("coef_done")
        hi_done = sem("hi_done")
        lo_done = sem("lo_done")
        xbo_done = sem("xbo_done")
        xT_mm = sem("xT_mm")
        xT_cp = sem("xT_cp")
        hT_mm = sem("hT_mm")
        hT_cp = sem("hT_cp")
        q_mm = sem("q_mm")
        q_cp = sem("q_cp")
        k_mm = sem("k_mm")
        k_cp = sem("k_cp")
        v_mm = sem("v_mm")
        v_cp = sem("v_cp")
        part_cp = [sem(f"part_cp{a}") for a in range(PARTS)]
        rest_done = sem("rest_done")
        q_out = [sem(f"q_out{p}") for p in range(PAIRS)]
        k_out = [sem(f"k_out{p}") for p in range(PAIRS)]
        q_in = [sem(f"q_in{p}") for p in range(PAIRS)]
        k_in = [sem(f"k_in{p}") for p in range(PAIRS)]
        stack_in = [sem("stack_in0"), sem("stack_in1")]
        v_staged = sem("v_staged")
        s_done = sem("s_done")
        max_done = sem("max_done")
        exp_done = sem("exp_done")
        pT_done = sem("pT_done")
        pT_cp = sem("pT_cp")
        av_done = sem("av_done")
        yraw_cp = sem("yraw_cp")
        inv_done = sem("inv_done")
        ytr_done = sem("ytr_done")
        ynorm_done = sem("ynorm_done")
        yT_mm = sem("yT_mm")
        yT_cp = sem("yT_cp")
        o_done = sem("o_done")
        x1_done = sem("x1_done")
        x1_edges = sem("x1_edges")
        lap_done = sem("lap_done")
        side_done = sem("side_done")
        coef_staged = sem("coef_staged")
        k_masked = sem("k_masked")
        react_done = sem("react_done")
        rx_done = sem("rx_done")
        dup_done = sem("dup_done")
        du_done = sem("du_done")
        duT_mm = sem("duT_mm")
        duT_cp = sem("duT_cp")
        duh_cp = sem("duh_cp")
        dul_cp = sem("dul_cp")
        lg_mm = sem("lg_mm")
        top_done = sem("top_done")
        index_done = sem("index_done")
        index_f = sem("index_f")
        gate2_done = sem("gate2_done")
        compared = sem("compared")
        picked = sem("picked")
        gates_done = sem("gates_done")
        gap_done = sem("gap_done")
        gap_tanh = sem("gap_tanh")
        uv_done = sem("uv_done")
        tanh_done = sem("tanh_done")
        silu_done = sem("silu_done")
        hid_done = sem("hid_done")
        y_done = sem("y_done")
        acc_done = sem("acc_done")
        out_done = sem("out_done")

        block = ctx.enter_context(nc.Block())

        @block.sync
        def _(sp):
            def gather_weights(half):
                for b in range(HALF * half, HALF * half + HALF):
                    cat = sp.value_load(cat_row[0:1, b:b + 1], min_val=0, max_val=CATS - 1)
                    sp.dma_start(cond_w_sb[:, b, :], cond_w[bass.ds(cat, 1), :, :].rearrange("a d h -> (a d) h"))\
                      .then_inc(in_cond_w[b], 16)

            def through_dram(p):
                for a in range(PARTS):
                    sp.wait_ge(part_cp[a], p)
                    sp.dma_start(q_trip[p, a].rearrange("d h t -> h d t"), qk_parts[:, p, a, 0, :])\
                      .then_inc(q_out[p], 16)
                    for row in ([a, a + PARTS] if a < PARTS - 1 else [a]):
                        sp.dma_start(k_trip[p, row].rearrange("d h t -> h d t"), qk_parts[:, p, a, 1, :])\
                          .then_inc(k_out[p], 16)
                sp.wait_ge(q_out[p], 16 * PARTS)
                sp.dma_start(stack_of(p, 0), q_trip[p].rearrange("(g a) d h t -> g (a d) h t", g=1)
                             .to_broadcast([PARTS, PARTS * DH, H, 2 * T])).then_inc(q_in[p], 16)
                sp.wait_ge(k_out[p], 16 * (2 * PARTS - 1))
                row = H * 2 * T
                first = k_trip[p]
                sp.dma_start(stack_of(p, 1),
                             bass.AP(first.tensor, first.offset, [[DH * row, PARTS], [row, PARTS * DH], [1, row]]))\
                  .then_inc(k_in[p], 16)

            def stage_stack(f, b):
                sp.dma_start(stack[:, :, :, T * b:T * b + T],
                             stack_kept[:, bass.ds(f, 1), :, :, T * b:T * b + T]
                             .rearrange("k p i h t -> k (p i) h t")).then_inc(stack_in[b], 16)

            def store(f):
                sp.wait_ge(acc_done, E * f + E)
                sp.dma_start(out[bass.ds(2 * f, 2)].rearrange("b t d -> t b d"), result[:, :, :])\
                  .then_inc(out_done, 16)

            sp.dma_start(cat_row[:, :], category.rearrange("(a b) -> a b", a=1)).then_inc(in_cat, 16)
            sp.dma_start(x_nat[:, 0:HALF, :], x[0:HALF].rearrange("b t d -> t b d")).then_inc(in_x[0], 16)
            sp.wait_ge(in_cat, 16)
            gather_weights(0)
            sp.dma_start(x_nat[:, HALF:B, :], x[HALF:B].rearrange("b t d -> t b d")).then_inc(in_x[1], 16)
            gather_weights(1)
            for i, w in enumerate((w1, w2)):
                sp.dma_start(w12_nat[:, i, :, :], w.rearrange("e d h -> d e h")).then_inc(in_w12[i], 16)
            through_dram(1)
            sp.dma_start(w3_sb[:, :, :, :], w3.rearrange("e (c h) d -> h e c d", c=2)).then_inc(in_w3, 16)
            for p in range(2, PAIRS):
                through_dram(p)
            for p in range(2, PAIRS):
                sp.wait_ge(k_in[p], 16)
                sp.wait_ge(q_in[p], 16)
            with sp.Fori(0, PAIRS - 2) as f:
                for b in range(2):
                    sp.wait_ge(s_done, GROUPS * f + GROUPS + QR * (b + 1))
                    stage_stack(f, b)
                store(f)
            store(PAIRS - 2)
            store(PAIRS - 1)
            sp.wait_ge(out_done, 16 * PAIRS + 1)

        @block.gpsimd
        def _(pool):
            pool.memset(ident[:, :], 0.0).then_inc(c_id, 1)
            pool.wait_ge(c_id, 1)
            pool.affine_select(out=ident[:, :], in_=ident[:, :], compare_op=ALU.not_equal, fill=1.0,
                               base=0, pattern=[[-1, 128]], channel_multiplier=1).then_inc(c_id, 1)
            pool.dma_start(cat_i[:, :], category.rearrange("(a b) -> a b", a=1).to_broadcast([CATS, B]))\
                .then_inc(in_cond_b, 16)
            pool.dma_start(cond_b_sb[:, :], cond_b).then_inc(in_cond_b, 16)
            pool.iota(part_i[:, :], pattern=[[0, 1]], base=0, channel_multiplier=1).then_inc(c_iota, 1)
            pool.iota(expert_i[:, :, :], pattern=[[0, 4], [1, E]], base=0, channel_multiplier=0).then_inc(c_iota, 1)
            pool.memset(head_rows[:, :], 1.0).then_inc(c_heads, 1)
            pool.wait_ge(c_heads, 1)
            pool.affine_select(out=head_rows[:, :], in_=head_rows[:, :], compare_op=ALU.is_ge, fill=0.0,
                               base=0, pattern=[[-DH, H]], channel_multiplier=1).then_inc(c_heads, 1)
            pool.wait_ge(c_heads, 2)
            pool.affine_select(out=head_rows[:, :], in_=head_rows[:, :], compare_op=ALU.is_ge, fill=0.0,
                               base=DH - 1, pattern=[[DH, H]], channel_multiplier=-1).then_inc(c_heads, 1)
            pool.memset(causal_b[:, :, :], 0.0).then_inc(c_causal, 1)
            pool.wait_ge(c_causal, 1)
            pool.affine_select(out=causal_b[:, :, :], in_=causal_b[:, :, :], compare_op=ALU.is_ge, fill=MASKED,
                               base=0, pattern=[[0, QC], [-1, T]], channel_multiplier=1).then_inc(c_causal, 1)
            pool.dma_start(bo_rows[:, :], bo.rearrange("(a d) -> a d", a=1).to_broadcast([T, D])).then_inc(in_rows, 16)
            for i, v in enumerate((coef_x, coef_y, coef_r)):
                pool.dma_start(coef_rows[:, i, :], v.rearrange("(a b) -> a b", a=1).to_broadcast([T, B]))\
                    .then_inc(in_coef, 16)
            pool.dma_start(w_gate_sb[:, :], w_gate).then_inc(in_gate, 16)

            def second_difference():
                pool.memset(stencil[:, :], 0.0).then_inc(c_stencil, 1)
                for n, (first, size, base, value) in enumerate(
                        [(0, T, 0, -2.0), (0, T, 1, 1.0), (0, T, -1, 1.0), (0, 1, -1, 2.0), (T - 1, 1, 2 - T, 2.0)]):
                    pool.wait_ge(c_stencil, n + 1)
                    cells = stencil[:, first:first + size]
                    pool.affine_select(out=cells, in_=cells, compare_op=ALU.not_equal, fill=value,
                                       base=base, pattern=[[-1, size]], channel_multiplier=1).then_inc(c_stencil, 1)

            def rests(p):
                pool.wait_ge(part_cp[0], p)
                if p > 1:
                    pool.wait_ge(part_cp[2], p - 1)
                pool.tensor_tensor(qk_rest[:, :, :], qk_all[:, p, :, :], qk_parts[:, p, 0, :, :], ALU.subtract)\
                    .then_inc(rest_done, 1)
                pool.wait_ge(part_cp[1], p)
                pool.tensor_tensor(qk_parts[:, p, 2, :, :], qk_rest[:, :, :], qk_parts[:, p, 1, :, :],
                                   ALU.subtract).then_inc(part_cp[2], 1)

            def stage_values(p, b):
                pool.wait_ge(av_done, GROUPS * p - GROUPS + QR * (b + 1))
                pool.tensor_copy(
                    v_pad[:, QC * b:QC * b + QC, :].rearrange("j c (r x) -> j c r x", x=32 + DH)[:, :, :, 0:DH],
                    v_all[:, bass.ds(p, 1), b, :].rearrange("j p (c r d) -> j (p c) r d", c=QC, r=QR))\
                    .then_inc(v_staged, 1)

            def diffusion_terms(p):
                pool.wait_ge(x1_edges, p + 1)
                pool.tensor_tensor(side_sum[:, :, :], x1[:, :, 0:D], x1[:, :, 2:D + 2], ALU.add)\
                    .then_inc(side_done, 1)
                for b in range(2):
                    last = pool.tensor_scalar(react[:, b, :], x1[:, b, 1:D + 1], coef_p[:, 2, b:b + 1],
                                              coef_p[:, 3, b:b + 1], ALU.mult, ALU.add)
                last.then_inc(react_done, 1)
                pool.wait_ge(react_done, p + 1)
                pool.tensor_tensor(react_x[:, :, :], react[:, :, :], x1[:, :, 1:D + 1], ALU.mult)\
                    .then_inc(rx_done, 1)

            def place_gates(f):
                if later(f):
                    pool.wait_ge(acc_done, E * f)
                pool.wait_ge(gate2_done, 2 * f + 2)
                pool.wait_ge(compared, f + 1)
                pool.tensor_tensor(pick[:, :, :, :].rearrange("t b k e -> t (b k) e"), same[:, :, :],
                                   gate2[:, :, :].rearrange("t b (k a) -> t (b k) a", a=1).to_broadcast([T, 4, E]),
                                   ALU.mult).then_inc(picked, 1)
                pool.wait_ge(picked, f + 1)
                pool.tensor_tensor(gates[:, :, :], pick[:, :, 0, :], pick[:, :, 1, :], ALU.add)\
                    .then_inc(gates_done, 1)

            rests(1)
            second_difference()
            pool.wait_ge(in_rows, 16)
            for half in range(2):
                pool.wait_ge(in_x[half], 16)
                for b in range(HALF * half, HALF * half + HALF):
                    last = pool.tensor_tensor(xbo_all[:, b // 2, b % 2, :], x_nat[:, b, :], bo_rows[:, :], ALU.add)
                last.then_inc(xbo_done, 1)
            rests(2)
            rests(3)
            for q in range(QC):
                pool.wait_ge(hi_done, q + 1)
                pool.tensor_tensor(w12_lo[:, 1, 2 * q:2 * q + 2, :], w12_nat[:, 1, 2 * q:2 * q + 2, :],
                                   w12_hi[:, 1, 2 * q:2 * q + 2, :].bitcast(F32), ALU.subtract).then_inc(lo_done, 1)
            for b in range(2):
                stage_values(1, b)
            diffusion_terms(0)
            place_gates(0)

            def body(f, ahead):
                if ahead:
                    for b in range(2):
                        stage_values(f + 2, b)
                diffusion_terms(f + 1)
                place_gates(f + 1)

            with pool.Fori(0, PAIRS - 2) as f:
                body(f, True)
            body(PAIRS - 2, False)

        @block.scalar
        def _(act):
            for i, w in enumerate((wq_lsr, wk_lsr)):
                act.dma_start(lsr_nat[:, i, :], w.rearrange("h d r -> (h d) r")).then_inc(in_lsr, 16)
            act.dma_start(wk_nat[:, :], wk).then_inc(in_wk, 16)
            act.dma_start(proj_w[:, 0, :], wq).then_inc(in_proj, 16)
            for i, v in enumerate((bk, bq, bv)):
                act.dma_start(cols_in[:, i:i + 1], v.rearrange("(p a) -> p a", a=1)).then_inc(in_cols, 16)
            act.dma_start(proj_w[:, 1, :], wv).then_inc(in_proj, 16)
            act.dma_start(proj_w[:, 2, :], wo).then_inc(in_wo, 16)

            def exps(p, g):
                G = GROUPS * p + g
                act.wait_ge(max_done, G + 1)
                if g >= 2 or later(p):
                    act.wait_ge(pT_done, G - 1)
                if g % QR == 0 and later(p):
                    act.wait_ge(inv_done, 2 * p - 1 + g // QR)
                for c in range(QC):
                    last = nc.scalar.activation(probs[:, g % 2, c, :], ps_s[g % 2][:, T * c:T * c + T], ACT.Exp,
                                                bias=neg_max[:, g % 2, c:c + 1],
                                                accum_out=row_sum[:, g // QR, c, g % QR:g % QR + 1])
                last.then_inc(exp_done, 1)

            def copy_probsT(p, g):
                G = GROUPS * p + g
                act.wait_ge(pT_done, G + 1)
                if g >= 2 or later(p):
                    act.wait_ge(av_done, G - 1)
                nc.scalar.activation(probsT[:, g % 2, :, :], ps_t[:, :].rearrange("j (c i) -> j c i", c=QC), ACT.Copy)\
                    .then_inc(pT_cp, 1)

            def copy_yT(p):
                act.wait_ge(yT_mm, p + 1)
                nc.scalar.activation(yT[:, :, :], tail_bank(10).rearrange("h (b i) -> h b i", b=2), ACT.Identity,
                                     bias=cols_in[:, 2:3]).then_inc(yT_cp, 1)

            def copy_duT(p):
                act.wait_ge(duT_mm, p + 1)
                nc.scalar.activation(duT[:, :, :], tail_bank(14).rearrange("d (b s) -> d b s", b=2), ACT.Copy)\
                    .then_inc(duT_cp, 1)

            def tanh_slot(f, s):
                act.wait_ge(uv_done, SLOTS * f + s + 1)
                nc.scalar.activation(tanh_u[:, s % 2, :], ps_uv[s % 2][:, 0:2 * T], ACT.Tanh, scale=0.5)\
                    .then_inc(tanh_done, 1)

            def tanh_gap(f):
                act.wait_ge(gap_done, f + 1)
                nc.scalar.activation(gap_t[:, :], gap[:, :], ACT.Tanh, scale=0.5).then_inc(gap_tanh, 1)

            def copy_xT(half):
                act.wait_ge(xT_mm, half + 1)
                if half:
                    act.wait_ge(hT_mm, half)
                nc.scalar.activation(xT[:, :, :],
                                     ps_uv[0][:, :].rearrange("d (b t) -> d b t", b=HALF), ACT.Copy).then_inc(xT_cp, 1)

            def copy_q(half):
                act.wait_ge(q_mm, half + 1)
                nc.scalar.activation(qk_all[:, 2 * half:2 * half + 2, 0, :],
                                     ps_y[0][:, :].rearrange("h (p t) -> h p t", p=2), ACT.Identity,
                                     bias=cols_in[:, 1:2]).then_inc(q_cp, 1)

            def copy_v(half):
                act.wait_ge(v_mm, half + 1)
                nc.scalar.activation(v_all[:, 2 * half:2 * half + 2, :, :],
                                     ps_uv[0][:, :].rearrange("t (p b h) -> t p b h", p=2, b=2), ACT.Copy)\
                    .then_inc(v_cp, 1)

            def first_part(p):
                act.wait_ge(q_cp, p // 2 + 1)
                act.wait_ge(k_cp, p // 2 + 1)
                nc.scalar.activation(qk_parts[:, p, 0, :, :], qk_all[:, p, :, :], ACT.Copy).then_inc(part_cp[0], 1)

            def second_part(p):
                act.wait_ge(rest_done, p)
                nc.scalar.activation(qk_parts[:, p, 1, :, :], qk_rest[:, :, :], ACT.Copy).then_inc(part_cp[1], 1)

            def round_w12(q):
                if q == 0:
                    act.wait_ge(in_w12[0], 16)
                    act.wait_ge(in_w12[1], 16)
                nc.scalar.activation(w12_hi[:, :, 2 * q:2 * q + 2, :], w12_nat[:, :, 2 * q:2 * q + 2, :], ACT.Copy)\
                    .then_inc(hi_done, 1)

            act.wait_ge(lsr_tr, 1)
            nc.scalar.activation(lsrT[:, :, :], ps_s[1][0:RANK, 0:256].rearrange("r (i h) -> r i h", i=2), ACT.Copy)\
                .then_inc(lsr_cp, 1)
            copy_xT(0)
            act.wait_ge(in_cols, 48)
            copy_q(0)
            first_part(1)
            copy_v(0)
            second_part(1)
            fill = {1: [lambda: copy_xT(1)], 3: [lambda: copy_q(1)],
                    4: [lambda: copy_v(1), lambda: first_part(2), lambda: round_w12(0)],
                    5: [lambda: second_part(2), lambda: first_part(3), lambda: round_w12(1)],
                    6: [lambda: second_part(3), lambda: round_w12(2)], 7: [lambda: round_w12(3)]}
            for g in range(GROUPS):
                exps(0, g)
                for step in fill.get(g, []):
                    step()
            exps(1, 0)
            exps(1, 1)
            copy_probsT(1, 0)
            copy_yT(0)
            exps(1, 2)
            copy_probsT(1, 1)
            exps(1, 3)
            copy_probsT(1, 2)
            copy_duT(0)
            copy_probsT(1, 3)

            def body(f, ahead):
                for s in range(SLOTS):
                    if s == 11:
                        copy_yT(f + 1)
                    if s == 15:
                        copy_duT(f + 1)
                    tanh_slot(f, s)
                    if s == 0:
                        tanh_gap(f)
                    if group_at(f, s - 1, ahead):
                        exps(*group_at(f, s - 1, ahead))
                    if group_at(f, s - 2, ahead):
                        copy_probsT(*group_at(f, s - 2, ahead))

            with act.Fori(0, PAIRS - 2) as f:
                body(f, True)
            body(PAIRS - 2, False)
            for s in range(SLOTS):
                tanh_slot(PAIRS - 1, s)
                if s == 0:
                    tanh_gap(PAIRS - 1)

        @block.vector
        def _(dve):
            def row_max(p, g):
                dve.wait_ge(s_done, GROUPS * p + g + 1)
                nc.vector.tensor_reduce(neg_max[:, g % 2, :], ps_s[g % 2][:, :].rearrange("i (c j) -> i c j", c=QC),
                                        AX, ALU.max, negate=True).then_inc(max_done, 1)

            def copy_probsT(p, g):
                G = GROUPS * p + g
                dve.wait_ge(pT_done, G + 1)
                if g >= 2 or later(p):
                    dve.wait_ge(av_done, G - 1)
                nc.vector.tensor_copy(probsT[:, g % 2, :, :], ps_t[:, :].rearrange("j (c i) -> j c i", c=QC))\
                    .then_inc(pT_cp, 1)

            def stage_first_values():
                dve.wait_ge(c_zero, 1)
                dve.wait_ge(v_cp, 1)
                nc.vector.tensor_copy(
                    v_pad[:, :, :].rearrange("j n (r x) -> j n r x", r=QR)[:, :, :, 0:DH],
                    v_all[:, 0, :, :].rearrange("j b (c r d) -> j (b c) r d", c=QC, r=QR)).then_inc(v_staged, 2)

            def mask_keys(r):
                for c in range(QC):
                    h = QR * c + r
                    last = nc.vector.tensor_scalar(k_head[:, :, r, c, :],
                                                   qk_all[:, 0, 1, :].rearrange("k (b t) -> k b t", b=2),
                                                   head_rows[:, h:h + 1], None, ALU.mult)
                last.then_inc(k_masked, 1)

            def copy_yraw(p):
                dve.wait_ge(av_done, GROUPS * p + GROUPS)
                nc.vector.tensor_copy(yT_raw[:, :, :], ps_m[:, 0:2 * T].rearrange("h (b i) -> h b i", b=2))\
                    .then_inc(yraw_cp, 1)

            def invert_sums(p, b):
                dve.wait_ge(exp_done, GROUPS * p + QR * (b + 1))
                nc.vector.reciprocal(inv_sum[:, H * b:H * b + H], row_sum[:, b, :, :].rearrange("i c r -> i (c r)"))\
                    .then_inc(inv_done, 1)

            def norm_y(p):
                dve.wait_ge(ytr_done, p + 1)
                dve.wait_ge(inv_done, 2 * p + 2)
                nc.vector.tensor_tensor(
                    y_nat[:, :, :].rearrange("i b (h d) -> i (b h) d", h=H),
                    tail_bank(9).rearrange("i (n d) -> i n d", d=DH),
                    inv_sum[:, :].rearrange("i (n a) -> i n a", a=1).to_broadcast([T, 2 * H, DH]),
                    ALU.mult).then_inc(ynorm_done, 1)

            def first_residual(p):
                dve.wait_ge(o_done, p + 1)
                nc.vector.tensor_tensor(x1[:, :, 1:D + 1], tail_bank(11).rearrange("t (b d) -> t b d", b=2),
                                        xbo_all[:, bass.ds(p, 1), :, :].rearrange("t p b d -> t (p b) d"),
                                        ALU.add).then_inc(x1_done, 1)
                if later(p):
                    dve.wait_ge(react_done, p)
                nc.vector.tensor_copy(coef_p[:, :, :], coef[:, bass.ds(p, 1), :, :]
                                      .rearrange("t p k b -> t (p k) b")).then_inc(coef_staged, 1)
                dve.wait_ge(x1_done, p + 1)
                nc.vector.tensor_copy(x1[:, :, 0:D + 2:D + 1], x1[:, :, 2:D:D - 3]).then_inc(x1_edges, 1)

            def diffuse(p):
                dve.wait_ge(side_done, p + 1)
                dve.wait_ge(rx_done, p + 1)
                for b in range(2):
                    nc.vector.scalar_tensor_tensor(du_part[:, b, :], side_sum[:, b, :], coef_p[:, 0, b:b + 1],
                                                   react_x[:, b, :], ALU.mult, ALU.add).then_inc(dup_done, 1)
                dve.wait_ge(lap_done, p + 1)
                for b in range(2):
                    dve.wait_ge(dup_done, 2 * p + b + 1)
                    last = nc.vector.scalar_tensor_tensor(du[:, b, :], tail_bank(13)[:, D * b:D * b + D],
                                                          coef_p[:, 1, b:b + 1], du_part[:, b, :],
                                                          ALU.mult, ALU.add)
                last.then_inc(du_done, 1)

            def split_duT(p):
                if later(p):
                    dve.wait_ge(uv_done, SLOTS * p)
                dve.wait_ge(duT_cp, p + 1)
                flat = duT[:, :, :].rearrange("d b t -> d (b t)")
                nc.vector.tensor_copy(duT_hi[:, :], flat).then_inc(duh_cp, 1)
                dve.wait_ge(duh_cp, p + 1)
                nc.vector.tensor_tensor(duT_lo[:, :], flat, duT_hi[:, :].bitcast(F32), ALU.subtract)\
                    .then_inc(dul_cp, 1)

            def rank_experts(f):
                dve.wait_ge(lg_mm, f + 1)
                nc.vector.tensor_copy(logits[:, :, :], tail_bank(15)[:, 0:2 * E].rearrange("t (b e) -> t b e", b=2))
                for b in range(2):
                    last = nc.vector.max(top8[:, b, :], tail_bank(15)[:, E * b:E * b + E])
                last.then_inc(top_done, 1)
                dve.wait_ge(top_done, f + 1)
                nc.vector.tensor_tensor(gap[:, :].rearrange("t (b a) -> t b a", a=1), top8[:, :, 0:1],
                                        top8[:, :, 1:2], ALU.subtract).then_inc(gap_done, 1)
                for b in range(2):
                    last = nc.vector.max_index(top_i[:, b, :], top8[:, b, :], logits[:, b, :])
                last.then_inc(index_done, 1)
                dve.wait_ge(index_done, f + 1)
                nc.vector.tensor_copy(top_f[:, :, :], top_i[:, :, 0:2]).then_inc(index_f, 1)

            def weigh_experts(f):
                dve.wait_ge(index_f, f + 1)
                nc.vector.tensor_tensor(same[:, :, :], expert_f[:, :, :],
                                        top_f[:, :, :].rearrange("t b (k a) -> t (b k) a", a=1)
                                        .to_broadcast([T, 4, E]), ALU.is_equal).then_inc(compared, 1)
                dve.wait_ge(gap_tanh, f + 1)
                for k, sign in enumerate((0.25, -0.25)):
                    nc.vector.tensor_scalar(gate2[:, :, k:k + 1], gap_t[:, :].rearrange("t (b a) -> t b a", a=1),
                                            sign, 0.25, ALU.mult, ALU.add).then_inc(gate2_done, 1)
            def silu(f, s):
                dve.wait_ge(tanh_done, SLOTS * f + s + 1)
                nc.vector.scalar_tensor_tensor(silu_u[:, s % 2, :], tanh_u[:, s % 2, :], 1.0,
                                               ps_uv[s % 2][:, 0:2 * T], ALU.add, ALU.mult).then_inc(silu_done, 1)

            def gate_hidden(f, s):
                dve.wait_ge(silu_done, SLOTS * f + s + 1)
                nc.vector.tensor_tensor(hidden[:, s % 2, :, :].rearrange("h b t -> h (b t)"), silu_u[:, s % 2, :],
                                        ps_uv[s % 2][:, 2 * T:4 * T], ALU.mult).then_inc(hid_done, 1)

            def add_expert(f, e):
                dve.wait_ge(y_done, SLOTS * f + 2 * e + 2)
                if e == 0:
                    dve.wait_ge(gates_done, f + 1)
                else:
                    dve.wait_ge(acc_done, E * f + e)
                if e == E - 1:
                    dve.wait_ge(out_done, 16 * f + 1)
                for b in range(2):
                    base = x1[:, b, 1:D + 1] if e == 0 else acc[:, b, :]
                    into = result[:, b, :] if e == E - 1 else acc[:, b, :]
                    last = nc.vector.scalar_tensor_tensor(into, ps_y[e % 2][:, D * b:D * b + D],
                                                          gates[:, b, e:e + 1], base, ALU.mult, ALU.add)
                last.then_inc(acc_done, 1)

            def bias_h(half):
                dve.wait_ge(hT_mm, half + 1)
                part = slice(HALF * half, HALF * half + HALF)
                nc.vector.tensor_tensor(hT[:, part, :], ps_uv[1][:, :].rearrange("d (b t) -> d b t", b=HALF),
                                        cond_bias[:, part].rearrange("d (b a) -> d b a", a=1)
                                        .to_broadcast([D, HALF, T]), ALU.add).then_inc(hT_cp, 1)

            def bias_k(half):
                dve.wait_ge(k_mm, half + 1)
                nc.vector.tensor_scalar(qk_all[:, 2 * half:2 * half + 2, 1, :],
                                        ps_y[1][:, :].rearrange("h (p t) -> h p t", p=2), bk_fold[:, 0:1], None,
                                        ALU.add).then_inc(k_cp, 1)

            def w1_rest(q):
                dve.wait_ge(hi_done, q + 1)
                nc.vector.tensor_tensor(w12_lo[:, 0, 2 * q:2 * q + 2, :], w12_nat[:, 0, 2 * q:2 * q + 2, :],
                                        w12_hi[:, 0, 2 * q:2 * q + 2, :].bitcast(F32), ALU.subtract)\
                    .then_inc(lo_done, 1)

            nc.vector.memset(v_pad[:, :, :], 0.0).then_inc(c_zero, 1)
            nc.vector.memset(result[:, :, :], 0.0).then_inc(out_done, 1)
            dve.wait_ge(c_id, 2)
            nc.vector.tensor_copy(ident_b[:, :], ident[:, :]).then_inc(c_id, 1)
            dve.wait_ge(in_cond_b, 32)
            dve.wait_ge(c_iota, 2)
            nc.vector.tensor_copy(cat_f[:, :], cat_i[:, :]).then_inc(cast_done, 1)
            nc.vector.tensor_copy(part_f[:, :], part_i[:, :]).then_inc(cast_done, 1)
            nc.vector.tensor_copy(expert_f[:, :, :], expert_i[:, :, :]).then_inc(cast_done, 1)
            dve.wait_ge(cast_done, 3)
            nc.vector.tensor_scalar(onehot[:, :], cat_f[:, :], part_f[:, 0:1], None, ALU.is_equal)\
                .then_inc(onehot_done, 1)
            dve.wait_ge(proj_tr, 1)
            nc.vector.tensor_copy(proj_wT[:, 0:2, :], ps_s[0][:, 0:256].rearrange("d (i h) -> d i h", i=2))\
                .then_inc(proj_cp, 1)
            dve.wait_ge(fold_mm, 1)
            dve.wait_ge(c_heads, 3)
            nc.vector.scalar_tensor_tensor(
                fold[:, :].rearrange("k (h d) -> k h d", h=H), ps_t[:, 0:128].rearrange("k (h d) -> k h d", h=H), SCALE,
                head_rows[:, :].rearrange("k (h a) -> k h a", a=1).to_broadcast([128, H, DH]), ALU.mult, ALU.mult)\
                .then_inc(fold_cp, 1)
            dve.wait_ge(cb_mm, 1)
            nc.vector.tensor_copy(cond_bias[:, :], ps_y[0][:, 0:B]).then_inc(cb_cp, 1)
            dve.wait_ge(cb_cp, 1)
            bias_h(0)
            dve.wait_ge(wk_mm, 1)
            nc.vector.tensor_copy(wkT[:, :], ps_y[1][:, 0:128]).then_inc(wk_cp, 1)
            nc.vector.tensor_copy(bk_fold[:, :], ps_y[1][:, 128:129]).then_inc(wk_cp, 1)
            dve.wait_ge(wk_cp, 2)
            bias_k(0)
            dve.wait_ge(k_cp, 1)
            mask_keys(0)
            mask_keys(1)
            dve.wait_ge(wo_tr, 1)
            nc.vector.tensor_copy(proj_wT[:, 2, :], ps_m[:, 0:128]).then_inc(wo_cp, 1)

            def prepare_coefficients():
                def rows(i):
                    return coef_rows[:, i, :].rearrange("t (p b) -> t p b", b=2)

                dve.wait_ge(in_coef, 48)
                nc.vector.tensor_copy(coef[:, :, 0, :], rows(0)).then_inc(coef_done, 1)
                nc.vector.tensor_copy(coef[:, :, 1, :], rows(1)).then_inc(coef_done, 1)
                nc.vector.tensor_scalar(coef[:, :, 2, :], rows(2), -1.0, None, ALU.mult).then_inc(coef_done, 1)
                nc.vector.scalar_tensor_tensor(coef[:, :, 3, :], rows(0), -2.0, rows(2), ALU.mult, ALU.add)\
                    .then_inc(coef_done, 1)

            fill = {0: lambda: mask_keys(2), 1: lambda: (mask_keys(3), stage_first_values()), 2: lambda: bias_h(1),
                    4: lambda: bias_k(1), 5: lambda: (prepare_coefficients(), w1_rest(0)),
                    6: lambda: w1_rest(1), 7: lambda: w1_rest(2)}
            for g in range(GROUPS):
                row_max(0, g)
                if g >= 2:
                    copy_probsT(0, g - 2)
                if g == QR:
                    invert_sums(0, 0)
                if g in fill:
                    fill[g]()
            row_max(1, 0)
            copy_probsT(0, GROUPS - 2)
            w1_rest(3)
            row_max(1, 1)
            copy_probsT(0, GROUPS - 1)
            invert_sums(0, 1)
            copy_yraw(0)
            norm_y(0)
            row_max(1, 2)
            dve.wait_ge(xbo_done, 2)
            dve.wait_ge(coef_done, 4)
            first_residual(0)
            row_max(1, 3)
            diffuse(0)
            invert_sums(1, 0)
            row_max(1, 4)
            split_duT(0)

            def body(f, ahead):
                for s in range(SLOTS):
                    if s >= 3 and s % 2 == 1:
                        add_expert(f, (s - 3) // 2)
                    if s >= 2 and s % 2 == 0 and group_at(f, s - 1, ahead):
                        row_max(*group_at(f, s - 1, ahead))
                    if s == 8:
                        invert_sums(f + 1, 1)
                    if s == 9:
                        copy_yraw(f + 1)
                    if s == 10:
                        norm_y(f + 1)
                    if s == 12:
                        first_residual(f + 1)
                    if s == 14:
                        diffuse(f + 1)
                    if s == SLOTS - 1:
                        split_duT(f + 1)
                    silu(f, s)
                    gate_hidden(f, s)
                    if s == 0:
                        rank_experts(f)
                    if s == 1:
                        weigh_experts(f)
                if ahead:
                    invert_sums(f + 2, 0)
                    row_max(f + 2, QR)
                add_expert(f, E - 1)

            with dve.Fori(0, PAIRS - 2) as f:
                body(f, True)
            body(PAIRS - 2, False)
            for s in range(SLOTS):
                if s >= 3 and s % 2 == 1:
                    add_expert(PAIRS - 1, (s - 3) // 2)
                silu(PAIRS - 1, s)
                gate_hidden(PAIRS - 1, s)
                if s == 0:
                    rank_experts(PAIRS - 1)
                if s == 1:
                    weigh_experts(PAIRS - 1)
            add_expert(PAIRS - 1, E - 1)

        @block.tensor
        def _(pe):
            mm = nc.tensor.matmul

            def transpose_x(half):
                pe.wait_ge(in_x[half], 16)
                if half:
                    pe.wait_ge(v_cp, half)
                for b in range(HALF):
                    last = nc.tensor.transpose(ps_uv[0][:, T * b:T * b + T], x_nat[:, HALF * half + b, :], ident[:, :])
                last.then_inc(xT_mm, 1)

            def condition(half):
                pe.wait_ge(xT_cp, half + 1)
                if half:
                    pe.wait_ge(hT_cp, half)
                for b in range(HALF):
                    pe.wait_ge(in_cond_w[HALF * half + b], 16)
                    last = mm(ps_uv[1][:, T * b:T * b + T], cond_w_sb[:, HALF * half + b, :],
                              xT[:, b, :], start=True, stop=True)
                last.then_inc(hT_mm, 1)

            def project_q(half):
                pe.wait_ge(hT_cp, half + 1)
                if half:
                    pe.wait_ge(q_cp, half)
                mm(ps_y[0][:, :], proj_wT[:, 0, :], hT[:, HALF * half:HALF * half + HALF, :],
                   start=True, stop=True).then_inc(q_mm, 1)

            def project_k(half):
                if half:
                    pe.wait_ge(k_cp, half)
                mm(ps_y[1][:, :], wkT[:, :], hT[:, HALF * half:HALF * half + HALF, :],
                   start=True, stop=True).then_inc(k_mm, 1)

            def project_v(half):
                pe.wait_ge(xT_cp, half + 1)
                for b in range(HALF):
                    last = mm(ps_uv[0][:, D * b:D * b + D], hT[:, HALF * half + b, :], proj_wT[:, 1, :],
                              start=True, stop=True)
                last.then_inc(v_mm, 1)

            def scores(p, g):
                G = GROUPS * p + g
                b, r = g // QR, g % QR
                first_pair = isinstance(p, int) and p == 0
                if first_pair:
                    pe.wait_ge(q_cp, 1)
                    pe.wait_ge(k_masked, r + 1)
                elif isinstance(p, int) and p == 1:
                    if g == 0:
                        pe.wait_ge(q_in[1], 16)
                        pe.wait_ge(k_in[1], 16)
                elif r == 0:
                    pe.wait_ge(stack_in[b], 16 * (p - 1))
                if g >= 2 or later(p):
                    pe.wait_ge(exp_done, G - 1)
                if later(p) and 2 <= g <= 5:
                    pe.wait_ge({2: yT_cp, 3: x1_done, 4: duT_cp, 5: top_done}[g], p)
                mm(ps_s[g % 2][:, :], ident_b[:, :], causal_b[:, :, :], start=True, stop=False, skip_group_check=True)
                if first_pair:
                    last = mm(ps_s[g % 2][:, :], qk_all[:, 0, 0, T * b:T * b + T], k_head[:, b, r, :, :],
                              start=False, stop=True, skip_group_check=True)
                else:
                    for c in range(QC):
                        h = QR * c + r
                        last = mm(ps_s[g % 2][:, T * c:T * c + T], stack[:, 0, h, T * b:T * b + T],
                                  stack[:, 1, h, T * b:T * b + T],
                                  start=False, stop=True, skip_group_check=True)
                last.then_inc(s_done, 1)

            def transpose_probs(p, g):
                G = GROUPS * p + g
                pe.wait_ge(exp_done, G + 1)
                if g >= 1 or later(p):
                    pe.wait_ge(pT_cp, G)
                for c in range(QC):
                    last = nc.tensor.transpose(ps_t[:, T * c:T * c + T], probs[:, g % 2, c, :], ident[:, :])
                last.then_inc(pT_done, 1)

            def weigh_values(p, g):
                b, r = g // QR, g % QR
                pe.wait_ge(pT_cp, GROUPS * p + g + 1)
                if r == 0:
                    pe.wait_ge(v_staged, 2 * p + b + 1)
                if g == 0 and later(p):
                    pe.wait_ge(yraw_cp, p)
                for c in range(QC):
                    last = mm(ps_m[32 * c:32 * c + 32, T * b:T * b + T], v_pad[:, QC * b + c, 32 * r:32 * r + 32],
                              probsT[:, g % 2, c, :], start=r == 0, stop=r == QR - 1)
                last.then_inc(av_done, 1)

            def transpose_y(p):
                pe.wait_ge(yraw_cp, p + 1)
                for b in range(2):
                    last = nc.tensor.transpose(tail_bank(9)[:, D * b:D * b + D], yT_raw[:, b, :], ident[:, :])
                last.then_inc(ytr_done, 1)

            def transpose_y_back(p):
                pe.wait_ge(ynorm_done, p + 1)
                for b in range(2):
                    last = nc.tensor.transpose(tail_bank(10)[:, T * b:T * b + T], y_nat[:, b, :], ident[:, :])
                last.then_inc(yT_mm, 1)

            def project_out(p):
                pe.wait_ge(yT_cp, p + 1)
                for b in range(2):
                    last = mm(tail_bank(11)[:, D * b:D * b + D], yT[:, b, :], proj_wT[:, 2, :], start=True, stop=True)
                last.then_inc(o_done, 1)

            def laplace_tokens(p):
                pe.wait_ge(x1_done, p + 1)
                mm(tail_bank(13), stencil[:, :], x1[:, :, 1:D + 1], start=True, stop=True).then_inc(lap_done, 1)

            def transpose_du(p):
                pe.wait_ge(du_done, p + 1)
                for b in range(2):
                    last = nc.tensor.transpose(tail_bank(14)[:, T * b:T * b + T], du[:, b, :], ident[:, :])
                last.then_inc(duT_mm, 1)

            def score_experts(p):
                pe.wait_ge(duT_cp, p + 1)
                for b in range(2):
                    last = mm(tail_bank(15)[:, E * b:E * b + E], duT[:, b, :], w_gate_sb[:, :], start=True, stop=True)
                last.then_inc(lg_mm, 1)

            def expert_up(f, s):
                e, c = s // 2, s % 2
                if s == 0:
                    pe.wait_ge(dul_cp, f + 1)
                if s >= 2:
                    pe.wait_ge(hid_done, SLOTS * f + s - 1)
                for i in range(2):
                    w_hi = w12_hi[:, i, e, 128 * c:128 * c + 128]
                    w_lo = w12_lo[:, i, e, 128 * c:128 * c + 128]
                    into = ps_uv[s % 2][:, 2 * T * i:2 * T * i + 2 * T]
                    mm(into, w_hi, duT_hi[:, :], start=True, stop=False)
                    mm(into, w_hi, duT_lo[:, :], start=False, stop=False)
                    last = mm(into, w_lo, duT_hi[:, :], start=False, stop=True)
                last.then_inc(uv_done, 1)

            def expert_down(f, s):
                e, c = s // 2, s % 2
                pe.wait_ge(hid_done, SLOTS * f + s + 1)
                if c == 0 and e >= 2:
                    pe.wait_ge(acc_done, E * f + e - 1)
                for b in range(2):
                    last = mm(ps_y[e % 2][:, D * b:D * b + D], hidden[:, s % 2, b, :], w3_sb[:, e, c, :],
                              start=c == 0 and b == 0, stop=c == 1, skip_group_check=True)
                last.then_inc(y_done, 1)

            pe.wait_ge(c_id, 2)
            pe.wait_ge(in_lsr, 32)
            for i in range(2):
                last = nc.tensor.transpose(ps_s[1][0:RANK, 128 * i:128 * i + 128], lsr_nat[:, i, :], ident[:, :])
            last.then_inc(lsr_tr, 1)
            transpose_x(0)
            pe.wait_ge(lsr_cp, 1)
            mm(ps_t[:, 0:128], lsrT[:, 1, :], lsrT[:, 0, :], start=True, stop=True).then_inc(fold_mm, 1)
            pe.wait_ge(in_proj, 32)
            for i in range(2):
                last = nc.tensor.transpose(ps_s[0][:, 128 * i:128 * i + 128], proj_w[:, i, :], ident[:, :])
            last.then_inc(proj_tr, 1)
            pe.wait_ge(onehot_done, 1)
            mm(ps_y[0][:, 0:B], cond_b_sb[:, :], onehot[:, :], start=True, stop=True).then_inc(cb_mm, 1)
            condition(0)
            pe.wait_ge(fold_cp, 1)
            pe.wait_ge(in_wk, 16)
            pe.wait_ge(in_cols, 48)
            mm(ps_y[1][:, 0:128], wk_nat[:, :], fold[:, :], start=True, stop=True)
            mm(ps_y[1][:, 128:129], fold[:, :], cols_in[:, 0:1], start=True, stop=True).then_inc(wk_mm, 1)
            pe.wait_ge(proj_cp, 1)
            pe.wait_ge(cb_cp, 1)
            project_q(0)
            pe.wait_ge(wk_cp, 2)
            project_k(0)
            project_v(0)
            pe.wait_ge(in_wo, 16)
            nc.tensor.transpose(ps_m[:, 0:128], proj_w[:, 2, :], ident[:, :]).then_inc(wo_tr, 1)
            pe.wait_ge(c_id, 3)
            pe.wait_ge(c_causal, 2)
            for g in range(GROUPS + 1):
                scores(g // GROUPS, g % GROUPS)
                if g == 1:
                    transpose_x(1)
                if g == 2:
                    condition(1)
                if g == 3:
                    project_q(1)
                    project_k(1)
                if g == 4:
                    project_v(1)
                if g >= 2:
                    transpose_probs(0, g - 2)
                if g == 3:
                    pe.wait_ge(wo_cp, 1)
                if g >= 3:
                    weigh_values(0, g - 3)
            scores(1, 1)
            transpose_probs(0, GROUPS - 1)
            weigh_values(0, GROUPS - 2)
            weigh_values(0, GROUPS - 1)
            transpose_probs(1, 0)
            transpose_y(0)
            weigh_values(1, 0)
            transpose_y_back(0)
            scores(1, 2)
            transpose_probs(1, 1)
            project_out(0)
            weigh_values(1, 1)
            scores(1, 3)
            transpose_probs(1, 2)
            pe.wait_ge(c_stencil, 6)
            laplace_tokens(0)
            weigh_values(1, 2)
            transpose_du(0)
            scores(1, 4)
            transpose_probs(1, 3)
            pe.wait_ge(in_gate, 16)
            score_experts(0)
            pe.wait_ge(lo_done, 2 * QC)
            pe.wait_ge(in_w3, 16)

            def body(f, ahead):
                for s in range(SLOTS):
                    expert_up(f, s)
                    if group_at(f, s, ahead):
                        scores(*group_at(f, s, ahead))
                    if s >= 1:
                        expert_down(f, s - 1)
                    if group_at(f, s - 2, ahead):
                        transpose_probs(*group_at(f, s - 2, ahead))
                    if group_at(f, s - 3, ahead):
                        weigh_values(*group_at(f, s - 3, ahead))
                    if s == 9:
                        transpose_y(f + 1)
                    if s == 10:
                        transpose_y_back(f + 1)
                    if s == 11:
                        project_out(f + 1)
                    if s == 13:
                        laplace_tokens(f + 1)
                    if s == 14:
                        transpose_du(f + 1)
                    if s == SLOTS - 1:
                        score_experts(f + 1)
                expert_down(f, SLOTS - 1)

            with pe.Fori(0, PAIRS - 2) as f:
                body(f, True)
            body(PAIRS - 2, False)
            for s in range(SLOTS):
                expert_up(PAIRS - 1, s)
                if s >= 1:
                    expert_down(PAIRS - 1, s - 1)
            expert_down(PAIRS - 1, SLOTS - 1)


_INS = ["x", "itok_B_0_63", "condB_zX", "condB_zY", "condB_zR", "L0_cond_W", "L0_cond_b", "L0_attn_Wq", "L0_attn_bq",
        "L0_attn_Wk", "L0_attn_bk", "L0_attn_Wv", "L0_attn_bv", "L0_attn_Wo", "L0_attn_bo", "L0_attn_Wq_lsr",
        "L0_attn_Wk_lsr", "L0_ffn_Wg", "L0_ffn_W1", "L0_ffn_W2", "L0_ffn_W3"]
_OUT = ((8, 128, 128), "float32")


def kernel(**inputs):
    import numpy as _np
    import concourse.bacc as _bacc
    from concourse import mybir as _mybir
    from concourse.bass_utils import run_bass_kernel_spmd as _run

    nc = _bacc.Bacc("TRN2", target_bir_lowering=False, num_devices=1)
    arrays, args = {}, []
    for name in _INS:
        a = _np.ascontiguousarray(inputs[name])
        arrays[f"in_{name}_dram"] = a
        args.append(nc.dram_tensor(f"in_{name}_dram", a.shape, _mybir.dt.from_np(a.dtype), kind="ExternalInput").ap())
    shape, dtype = _OUT
    args.append(nc.dram_tensor("out_dram", shape, _mybir.dt.from_np(_np.dtype(dtype)), kind="ExternalOutput").ap())
    adaln_attention_reaction_moe(nc, *args)
    r = _run(nc, [arrays], core_ids=[0])
    return r.results[0]["out_dram"]
```

```python
import concourse.bass as bass
from concourse import mybir
from contextlib import ExitStack


def adaln_attention_reaction_moe(
    nc: bass.Bass,
    x: bass.AP,
    category: bass.AP,
    coef_x: bass.AP,
    coef_y: bass.AP,
    coef_r: bass.AP,
    cond_w: bass.AP,
    cond_b: bass.AP,
    wq: bass.AP,
    bq: bass.AP,
    wk: bass.AP,
    bk: bass.AP,
    wv: bass.AP,
    bv: bass.AP,
    wo: bass.AP,
    bo: bass.AP,
    wq_lsr: bass.AP,
    wk_lsr: bass.AP,
    w_gate: bass.AP,
    w1: bass.AP,
    w2: bass.AP,
    w3: bass.AP,
    out: bass.AP,
):
    F32 = mybir.dt.float32
    F32R = mybir.dt.float32r
    BF16 = mybir.dt.bfloat16
    I32 = mybir.dt.int32
    U32 = mybir.dt.uint32
    ALU = mybir.AluOpType
    ACT = mybir.ActivationFunctionType
    AX = mybir.AxisListType.X

    B, T, D = x.shape
    CATS = cond_w.shape[0]
    H, DH, RANK = wq_lsr.shape
    E, _, HID = w1.shape
    PAIRS = B // 2
    HALF = B // 2
    QR = 4
    QC = H // QR
    SLOTS = 2 * E
    GROUPS = 2 * QR
    PARTS = 3
    STACK = PARTS * PARTS * DH
    SCALE = float(RANK) ** -0.5
    MASKED = -1e30
    assert D == T == H * DH == 128 and HID == 256 and B == 8 and QC == 4

    ctx = ExitStack()
    with ctx:
        def sb(name, shape, dt=F32):
            return ctx.enter_context(nc.sbuf_tensor(name, shape, dt))

        def pb(name):
            return ctx.enter_context(nc.psum_tensor(name, [128, 512], F32))

        def sem(name):
            return ctx.enter_context(nc.semaphore(name))

        def stack_of(p, i):
            return stack[:, i, :, :] if p == 1 else stack_kept[:, p - 2, i, :, :]

        def group_at(f, s, ahead):
            n = (s + 9) // 2
            if s % 2 == 0 or (n >= GROUPS and not ahead):
                return None
            return (f + 1, n) if n < GROUPS else (f + 2, n - GROUPS)

        def tail_bank(p, s):
            if isinstance(p, int) and p == 0 and s < SLOTS - 1:
                return ps_y[s % 2][:, 0:2 * T]
            return ps_s[(s // 2 + s % 2 + 1) % 2][:, 0:2 * T]

        def roomy(f, s):
            return isinstance(f, int) and SLOTS * f + s >= SLOTS * (PAIRS - 2) + 10

        def uv_bank(f, s):
            return (ps_uv + [ps_t, ps_m])[s % 4] if roomy(f, s) else ps_uv[s % 2]

        def hidden_of(f, s):
            ring = [hidden[:, 0, :, :], hidden[:, 1, :, :], k_head[:, 0, 0, 0:2, :], k_head[:, 0, 0, 2:4, :]]
            return ring[s % 4] if roomy(f, s) else ring[s % 2]

        def silu_of(f, s):
            ring = [silu_u[:, 0, :], silu_u[:, 1, :], k_head[:, 0, 1, 0:2, :].rearrange("h b t -> h (b t)")]
            return ring[(SLOTS * f + s + 2) % 3] if roomy(f, s) else ring[s % 2]

        def q_bank(half):
            return ps_uv[0] if half else ps_y[0]

        def k_bank(half):
            return ps_uv[1] if half else ps_y[1]

        def later(p):
            return not isinstance(p, int) or p > 0

        x_nat = sb("x_nat", [T, B, D])
        cond_w_sb = sb("cond_w_sb", [D, B, D])
        cond_b_sb = sb("cond_b_sb", [CATS, D])
        proj_w = sb("proj_w", [128, 3, D])
        wk_nat = sb("wk_nat", [128, D])
        lsr_nat = sb("lsr_nat", [128, 2, RANK])
        cols_in = sb("cols_in", [128, 3])
        bo_rows = sb("bo_rows", [T, D])
        cat_row = sb("cat_row", [1, B], I32)
        cat_i = sb("cat_i", [CATS, B], I32)
        coef_rows = sb("coef_rows", [T, 3, B])
        w_gate_sb = sb("w_gate_sb", [D, E])
        w12_nat = sb("w12_nat", [D, 2, E, HID])
        w3_sb = sb("w3_sb", [128, E, 2, D])
        ident = sb("ident", [128, 128])
        ident_b = sb("ident_b", [128, 128], BF16)
        causal_b = sb("causal_b", [T, QC, T], BF16)
        head_rows = sb("head_rows", [128, H])
        stencil = sb("stencil", [T, T])
        part_i = sb("part_i", [CATS, 1], I32)
        part_f = sb("part_f", [CATS, 1])
        expert_i = sb("expert_i", [T, 4, E], I32)
        expert_f = sb("expert_f", [T, 4, E])
        proj_wT = sb("proj_wT", [D, 3, 128])
        lsrT = sb("lsrT", [RANK, 2, 128])
        fold = sb("fold", [128, 128])
        wkT = sb("wkT", [D, 128])
        bk_fold = sb("bk_fold", [128, 1])
        cat_f = sb("cat_f", [CATS, B])
        onehot = sb("onehot", [CATS, B])
        cond_bias = sb("cond_bias", [D, B])
        w12_hi = sb("w12_hi", [D, 2, E, HID], F32R)
        w12_lo = sb("w12_lo", [D, 2, E, HID], F32R)
        coef = sb("coef", [T, PAIRS, 4, 2])
        xT = sb("xT", [D, HALF, T])
        hT = sb("hT", [D, B, T])
        qk_all = sb("qk_all", [128, PAIRS, 2, 2 * T])
        qk_parts = sb("qk_parts", [128, PAIRS, PARTS, 2, 2 * T], BF16)
        qk_rest = sb("qk_rest", [128, 2, 2 * T])
        k_head = sb("k_head", [128, 2, QR, QC, T])
        stack_kept = sb("stack_kept", [STACK, PAIRS - 2, 2, H, 2 * T], BF16)
        v_all = sb("v_all", [T, PAIRS, 2, D])
        xbo_all = sb("xbo_all", [T, PAIRS, 2, D])
        stack = sb("stack", [STACK, 2, H, 2 * T], BF16)
        v_pad = sb("v_pad", [T, 2 * QC, 160])
        coef_p = sb("coef_p", [T, 4, 2])
        neg_max = sb("neg_max", [T, 2, QC])
        probs = sb("probs", [T, 2, QC, T])
        row_sum = sb("row_sum", [T, 2, QC, QR])
        inv_sum = sb("inv_sum", [T, 2, H])
        inv_rep = sb("inv_rep", [T, 2, D])
        probsT = sb("probsT", [T, 2, QC, T])
        invT = sb("invT", [D, 2, T])
        yT = sb("yT", [128, 2, T])
        x1 = sb("x1", [T, 2, D + 2])
        side_sum = sb("side_sum", [T, 2, D])
        react = sb("react", [T, 2, D])
        react_x = sb("react_x", [T, 2, D])
        du_part = sb("du_part", [T, 2, D])
        du = sb("du", [T, 2, D])
        duT = sb("duT", [D, 2, T])
        duT_hi = sb("duT_hi", [D, 2 * T], F32R)
        duT_lo = sb("duT_lo", [D, 2 * T], F32R)
        logits = sb("logits", [T, 2, E])
        top8 = sb("top8", [T, 2, 8])
        top_i = sb("top_i", [T, 2, 8], U32)
        top_f = sb("top_f", [T, 2, 2])
        gap = sb("gap", [T, 2])
        gap_t = sb("gap_t", [T, 2])
        gate2 = sb("gate2", [T, 2, 2])
        same = sb("same", [T, 4, E])
        pick = sb("pick", [T, 2, 2, E])
        gates = sb("gates", [T, 2, E])
        tanh_u = sb("tanh_u", [128, 2, 2 * T])
        silu_u = sb("silu_u", [128, 2, 2 * T])
        hidden = sb("hidden", [128, 2, 2, T])
        acc = sb("acc", [T, 2, D])
        result = sb("result", [T, 2, D])

        q_trip = nc.dram_tensor("q_trip", [PAIRS, PARTS, DH, H, 2 * T], BF16).ap()
        k_trip = nc.dram_tensor("k_trip", [PAIRS, 2 * PARTS - 1, DH, H, 2 * T], BF16).ap()

        ps_uv = [pb("ps_uv0"), pb("ps_uv1")]
        ps_s = [pb("ps_s0"), pb("ps_s1")]
        ps_t = pb("ps_t")
        ps_y = [pb("ps_y0"), pb("ps_y1")]
        ps_m = pb("ps_m")

        in_x = [sem("in_x0"), sem("in_x1")]
        in_cat = sem("in_cat")
        in_cond_w = [sem(f"in_cond_w{b}") for b in range(B)]
        in_cond_b = sem("in_cond_b")
        in_proj = sem("in_proj")
        in_wo = sem("in_wo")
        in_wk = sem("in_wk")
        in_lsr = sem("in_lsr")
        in_cols = sem("in_cols")
        in_rows = sem("in_rows")
        in_coef = sem("in_coef")
        in_gate = sem("in_gate")
        in_w12 = [sem("in_w1"), sem("in_w2")]
        in_w3 = sem("in_w3")
        c_id = sem("c_id")
        c_causal = sem("c_causal")
        c_heads = sem("c_heads")
        c_stencil = sem("c_stencil")
        c_iota = sem("c_iota")
        c_zero = sem("c_zero")
        proj_tr = sem("proj_tr")
        proj_cp = sem("proj_cp")
        wo_tr = sem("wo_tr")
        wo_cp = sem("wo_cp")
        lsr_tr = sem("lsr_tr")
        lsr_cp = sem("lsr_cp")
        fold_mm = sem("fold_mm")
        fold_cp = sem("fold_cp")
        wk_mm = sem("wk_mm")
        wk_cp = sem("wk_cp")
        cast_done = sem("cast_done")
        onehot_done = sem("onehot_done")
        cb_mm = sem("cb_mm")
        cb_cp = sem("cb_cp")
        coef_done = sem("coef_done")
        hi_done = sem("hi_done")
        lo_done = sem("lo_done")
        xbo_done = sem("xbo_done")
        xT_mm = sem("xT_mm")
        xT_cp = sem("xT_cp")
        hT_mm = sem("hT_mm")
        hT_cp = sem("hT_cp")
        q_mm = sem("q_mm")
        q_cp = sem("q_cp")
        k_mm = sem("k_mm")
        k_cp = sem("k_cp")
        v_mm = sem("v_mm")
        v_cp = sem("v_cp")
        part_cp = [sem(f"part_cp{a}") for a in range(PARTS)]
        rest_done = sem("rest_done")
        q_out = [sem(f"q_out{p}") for p in range(PAIRS)]
        k_out = [sem(f"k_out{p}") for p in range(PAIRS)]
        q_in = [sem(f"q_in{p}") for p in range(PAIRS)]
        k_in = [sem(f"k_in{p}") for p in range(PAIRS)]
        stack_in = [sem("stack_in0"), sem("stack_in1")]
        v_staged = sem("v_staged")
        s_done = sem("s_done")
        max_done = sem("max_done")
        exp_done = sem("exp_done")
        pT_done = sem("pT_done")
        pT_cp = sem("pT_cp")
        av_done = sem("av_done")
        inv_done = sem("inv_done")
        inv_spread = sem("inv_spread")
        invT_mm = sem("invT_mm")
        invT_cp = sem("invT_cp")
        bv_mm = sem("bv_mm")
        bias_done = sem("bias_done")
        yT_cp = sem("yT_cp")
        o_done = sem("o_done")
        x1_done = sem("x1_done")
        x1_edges = sem("x1_edges")
        lap_done = sem("lap_done")
        side_done = sem("side_done")
        coef_staged = sem("coef_staged")
        k_masked = sem("k_masked")
        react_done = sem("react_done")
        rx_done = sem("rx_done")
        dup_done = sem("dup_done")
        du_done = sem("du_done")
        duT_mm = sem("duT_mm")
        duT_cp = sem("duT_cp")
        duh_cp = sem("duh_cp")
        dul_cp = sem("dul_cp")
        lg_mm = sem("lg_mm")
        top_done = sem("top_done")
        index_done = sem("index_done")
        index_f = sem("index_f")
        gate2_done = sem("gate2_done")
        compared = sem("compared")
        picked = sem("picked")
        gates_done = sem("gates_done")
        gap_done = sem("gap_done")
        gap_tanh = sem("gap_tanh")
        uv_done = sem("uv_done")
        tanh_done = sem("tanh_done")
        silu_done = sem("silu_done")
        hid_done = sem("hid_done")
        y_done = sem("y_done")
        acc_done = sem("acc_done")
        out_done = sem("out_done")

        block = ctx.enter_context(nc.Block())

        @block.sync
        def _(sp):
            def gather_weights(batches):
                for b in batches:
                    cat = sp.value_load(cat_row[0:1, b:b + 1], min_val=0, max_val=CATS - 1)
                    sp.dma_start(cond_w_sb[:, b, :], cond_w[bass.ds(cat, 1), :, :].rearrange("a d h -> (a d) h"))\
                      .then_inc(in_cond_w[b], 16)

            def through_dram(p):
                for a in range(PARTS):
                    sp.wait_ge(part_cp[a], p)
                    sp.dma_start(q_trip[p, a].rearrange("d h t -> h d t"), qk_parts[:, p, a, 0, :])\
                      .then_inc(q_out[p], 16)
                    for row in ([a, a + PARTS] if a < PARTS - 1 else [a]):
                        sp.dma_start(k_trip[p, row].rearrange("d h t -> h d t"), qk_parts[:, p, a, 1, :])\
                          .then_inc(k_out[p], 16)
                sp.wait_ge(q_out[p], 16 * PARTS)
                sp.dma_start(stack_of(p, 0), q_trip[p].rearrange("(g a) d h t -> g (a d) h t", g=1)
                             .to_broadcast([PARTS, PARTS * DH, H, 2 * T])).then_inc(q_in[p], 16)
                sp.wait_ge(k_out[p], 16 * (2 * PARTS - 1))
                row = H * 2 * T
                first = k_trip[p]
                sp.dma_start(stack_of(p, 1),
                             bass.AP(first.tensor, first.offset, [[DH * row, PARTS], [row, PARTS * DH], [1, row]]))\
                  .then_inc(k_in[p], 16)

            def stage_stack(p, b):
                sp.wait_ge(k_in[p], 16)
                sp.wait_ge(q_in[p], 16)
                sp.wait_ge(s_done, GROUPS * (p - 1) + QR * (b + 1))
                sp.dma_start(stack[:, :, :, T * b:T * b + T], stack_kept[:, p - 2, :, :, T * b:T * b + T])\
                  .then_inc(stack_in[b], 16)

            def store(f):
                sp.wait_ge(acc_done, E * f + E)
                sp.dma_start(out[2 * f:2 * f + 2].rearrange("b t d -> t b d"), result[:, :, :])\
                  .then_inc(out_done, 16)

            sp.dma_start(cat_row[:, :], category.rearrange("(a b) -> a b", a=1)).then_inc(in_cat, 16)
            sp.dma_start(x_nat[:, 0:HALF, :], x[0:HALF].rearrange("b t d -> t b d")).then_inc(in_x[0], 16)
            sp.wait_ge(in_cat, 16)
            gather_weights(range(2))
            sp.dma_start(x_nat[:, HALF:B, :], x[HALF:B].rearrange("b t d -> t b d")).then_inc(in_x[1], 16)
            gather_weights(range(HALF, B))
            for i, w in enumerate((w1, w2)):
                sp.dma_start(w12_nat[:, i, :, :], w.rearrange("e d h -> d e h")).then_inc(in_w12[i], 16)
            through_dram(1)
            sp.dma_start(w3_sb[:, :, :, :], w3.rearrange("e (c h) d -> h e c d", c=2)).then_inc(in_w3, 16)
            through_dram(2)
            stage_stack(2, 0)
            through_dram(3)
            stage_stack(2, 1)
            store(0)
            stage_stack(3, 0)
            stage_stack(3, 1)
            for f in range(1, PAIRS):
                store(f)
            sp.wait_ge(out_done, 16 * PAIRS + 1)

        @block.gpsimd
        def _(pool):
            pool.memset(ident[:, :], 0.0).then_inc(c_id, 1)
            pool.wait_ge(c_id, 1)
            pool.affine_select(out=ident[:, :], in_=ident[:, :], compare_op=ALU.not_equal, fill=1.0,
                               base=0, pattern=[[-1, 128]], channel_multiplier=1).then_inc(c_id, 1)
            pool.dma_start(cat_i[:, :], category.rearrange("(a b) -> a b", a=1).to_broadcast([CATS, B]))\
                .then_inc(in_cond_b, 16)
            pool.dma_start(cond_b_sb[:, :], cond_b).then_inc(in_cond_b, 16)
            pool.iota(part_i[:, :], pattern=[[0, 1]], base=0, channel_multiplier=1).then_inc(c_iota, 1)
            pool.iota(expert_i[:, :, :], pattern=[[0, 4], [1, E]], base=0, channel_multiplier=0).then_inc(c_iota, 1)
            for i, v in enumerate((bk, bq, bv)):
                pool.dma_start(cols_in[:, i:i + 1], v.rearrange("(p a) -> p a", a=1)).then_inc(in_cols, 16)
            pool.memset(head_rows[:, :], 1.0).then_inc(c_heads, 1)
            pool.wait_ge(c_heads, 1)
            pool.affine_select(out=head_rows[:, :], in_=head_rows[:, :], compare_op=ALU.is_ge, fill=0.0,
                               base=0, pattern=[[-DH, H]], channel_multiplier=1).then_inc(c_heads, 1)
            pool.wait_ge(c_heads, 2)
            pool.affine_select(out=head_rows[:, :], in_=head_rows[:, :], compare_op=ALU.is_ge, fill=0.0,
                               base=DH - 1, pattern=[[DH, H]], channel_multiplier=-1).then_inc(c_heads, 1)
            pool.memset(causal_b[:, :, :], 0.0).then_inc(c_causal, 1)
            pool.wait_ge(c_causal, 1)
            pool.affine_select(out=causal_b[:, :, :], in_=causal_b[:, :, :], compare_op=ALU.is_ge, fill=MASKED,
                               base=0, pattern=[[0, QC], [-1, T]], channel_multiplier=1).then_inc(c_causal, 1)
            pool.dma_start(bo_rows[:, :], bo.rearrange("(a d) -> a d", a=1).to_broadcast([T, D])).then_inc(in_rows, 16)
            for i, v in enumerate((coef_x, coef_y, coef_r)):
                pool.dma_start(coef_rows[:, i, :], v.rearrange("(a b) -> a b", a=1).to_broadcast([T, B]))\
                    .then_inc(in_coef, 16)
            pool.dma_start(w_gate_sb[:, :], w_gate).then_inc(in_gate, 16)

            def second_difference():
                pool.memset(stencil[:, :], 0.0).then_inc(c_stencil, 1)
                for n, (first, size, base, value) in enumerate(
                        [(0, T, 0, -2.0), (0, T, 1, 1.0), (0, T, -1, 1.0), (0, 1, -1, 2.0), (T - 1, 1, 2 - T, 2.0)]):
                    pool.wait_ge(c_stencil, n + 1)
                    cells = stencil[:, first:first + size]
                    pool.affine_select(out=cells, in_=cells, compare_op=ALU.not_equal, fill=value,
                                       base=base, pattern=[[-1, size]], channel_multiplier=1).then_inc(c_stencil, 1)

            def first_rest(p):
                pool.wait_ge(part_cp[0], p)
                if p > 1:
                    pool.wait_ge(part_cp[2], p - 1)
                pool.tensor_tensor(qk_rest[:, :, :], qk_all[:, p, :, :], qk_parts[:, p, 0, :, :], ALU.subtract)\
                    .then_inc(rest_done, 1)

            def third_part(p):
                pool.wait_ge(part_cp[1], p)
                pool.tensor_tensor(qk_parts[:, p, 2, :, :], qk_rest[:, :, :], qk_parts[:, p, 1, :, :],
                                   ALU.subtract).then_inc(part_cp[2], 1)

            def stage_values(p, b):
                pool.wait_ge(av_done, GROUPS * p - GROUPS + QR * (b + 1))
                pool.tensor_copy(
                    v_pad[:, QC * b:QC * b + QC, :].rearrange("j c (r x) -> j c r x", x=32 + DH)[:, :, :, 0:DH],
                    v_all[:, bass.ds(p, 1), b, :].rearrange("j p (c r d) -> j (p c) r d", c=QC, r=QR))\
                    .then_inc(v_staged, 1)

            def diffusion_terms(p):
                pool.wait_ge(x1_edges, p + 1)
                pool.tensor_tensor(side_sum[:, :, :], x1[:, :, 0:D], x1[:, :, 2:D + 2], ALU.add)\
                    .then_inc(side_done, 1)
                if not later(p):
                    return
                for b in range(2):
                    last = pool.tensor_scalar(react[:, b, :], x1[:, b, 1:D + 1], coef_p[:, 2, b:b + 1],
                                              coef_p[:, 3, b:b + 1], ALU.mult, ALU.add)
                last.then_inc(react_done, 1)
                pool.wait_ge(react_done, p + 1)
                pool.tensor_tensor(react_x[:, :, :], react[:, :, :], x1[:, :, 1:D + 1], ALU.mult)\
                    .then_inc(rx_done, 1)

            def place_gates(f):
                if later(f):
                    pool.wait_ge(acc_done, E * f)
                pool.wait_ge(gate2_done, 2 * f + 2)
                pool.wait_ge(compared, f + 1)
                pool.tensor_tensor(pick[:, :, :, :].rearrange("t b k e -> t (b k) e"), same[:, :, :],
                                   gate2[:, :, :].rearrange("t b (k a) -> t (b k) a", a=1).to_broadcast([T, 4, E]),
                                   ALU.mult).then_inc(picked, 1)
                pool.wait_ge(picked, f + 1)
                pool.tensor_tensor(gates[:, :, :], pick[:, :, 0, :], pick[:, :, 1, :], ALU.add)\
                    .then_inc(gates_done, 1)

            def w2_rest(q):
                pool.wait_ge(hi_done, q + 1)
                pool.tensor_tensor(w12_lo[:, 1, 2 * q:2 * q + 2, :], w12_nat[:, 1, 2 * q:2 * q + 2, :],
                                   w12_hi[:, 1, 2 * q:2 * q + 2, :].bitcast(F32), ALU.subtract).then_inc(lo_done, 1)

            first_rest(1)
            third_part(1)
            second_difference()
            pool.wait_ge(bias_done, 1)
            for half in range(2):
                pool.wait_ge(in_x[half], 16)
                for b in range(HALF * half, HALF * half + HALF):
                    last = pool.tensor_tensor(xbo_all[:, b // 2, b % 2, :], x_nat[:, b, :], bo_rows[:, :], ALU.add)
                last.then_inc(xbo_done, 1)
            w2_rest(0)
            w2_rest(1)
            first_rest(2)
            third_part(2)
            w2_rest(2)
            stage_values(1, 0)
            w2_rest(3)
            first_rest(3)
            diffusion_terms(0)
            third_part(3)
            stage_values(1, 1)
            place_gates(0)

            def body(f, ahead):
                if ahead:
                    for b in range(2):
                        stage_values(f + 2, b)
                diffusion_terms(f + 1)
                place_gates(f + 1)

            with pool.Fori(0, PAIRS - 2) as f:
                body(f, True)
            body(PAIRS - 2, False)

        @block.scalar
        def _(act):
            for i, w in enumerate((wq_lsr, wk_lsr)):
                act.dma_start(lsr_nat[:, i, :], w.rearrange("h d r -> (h d) r")).then_inc(in_lsr, 16)
            act.dma_start(wk_nat[:, :], wk).then_inc(in_wk, 16)
            act.dma_start(proj_w[:, 0, :], wq).then_inc(in_proj, 16)
            act.dma_start(proj_w[:, 1, :], wv).then_inc(in_proj, 16)
            act.wait_ge(in_cat, 16)
            for b in range(2, HALF):
                cat = act.value_load(cat_row[0:1, b:b + 1], min_val=0, max_val=CATS - 1)
                act.dma_start(cond_w_sb[:, b, :], cond_w[bass.ds(cat, 1), :, :].rearrange("a d h -> (a d) h"))\
                   .then_inc(in_cond_w[b], 16)

            def exps(p, g):
                G = GROUPS * p + g
                act.wait_ge(max_done, G + 1)
                if g >= 2 or later(p):
                    act.wait_ge(pT_done, G - 1)
                if g % QR == 0 and later(p):
                    act.wait_ge(inv_done, 2 * p - 1 + g // QR)
                for c in range(QC):
                    last = nc.scalar.activation(probs[:, g % 2, c, :], ps_s[g % 2][:, T * c:T * c + T], ACT.Exp,
                                                bias=neg_max[:, g % 2, c:c + 1],
                                                accum_out=row_sum[:, g // QR, c, g % QR:g % QR + 1])
                last.then_inc(exp_done, 1)

            def copy_probsT(p, g):
                G = GROUPS * p + g
                act.wait_ge(pT_done, G + 1)
                if g >= 2 or later(p):
                    act.wait_ge(av_done, G - 1)
                nc.scalar.activation(probsT[:, g % 2, :, :], ps_t[:, :].rearrange("j (c i) -> j c i", c=QC), ACT.Copy)\
                    .then_inc(pT_cp, 1)

            def copy_invT(p):
                act.wait_ge(invT_mm, p + 1)
                if later(p):
                    act.wait_ge(yT_cp, p)
                nc.scalar.activation(invT[:, :, :], tail_bank(p, 8).rearrange("h (b i) -> h b i", b=2), ACT.Copy)\
                    .then_inc(invT_cp, 1)

            def copy_duT(p):
                act.wait_ge(duT_mm, p + 1)
                nc.scalar.activation(duT[:, :, :], tail_bank(p, 14).rearrange("d (b s) -> d b s", b=2), ACT.Copy)\
                    .then_inc(duT_cp, 1)

            def tanh_slot(f, s):
                act.wait_ge(uv_done, SLOTS * f + s + 1)
                if s >= 2 or roomy(f, s):
                    act.wait_ge(silu_done, SLOTS * f + s - 1)
                nc.scalar.activation(tanh_u[:, s % 2, :], uv_bank(f, s)[:, 0:2 * T], ACT.Tanh, scale=0.5)\
                    .then_inc(tanh_done, 1)

            def tanh_gap(f):
                act.wait_ge(gap_done, f + 1)
                nc.scalar.activation(gap_t[:, :], gap[:, :], ACT.Tanh, scale=0.5).then_inc(gap_tanh, 1)

            def copy_second_xT():
                act.wait_ge(xT_mm, 2)
                act.wait_ge(hT_mm, 1)
                nc.scalar.activation(xT[:, :, :],
                                     ps_uv[0][:, :].rearrange("d (b t) -> d b t", b=HALF), ACT.Copy).then_inc(xT_cp, 1)

            def copy_q(half):
                act.wait_ge(q_mm, half + 1)
                nc.scalar.activation(qk_all[:, 2 * half:2 * half + 2, 0, :],
                                     q_bank(half)[:, :].rearrange("h (p t) -> h p t", p=2), ACT.Identity,
                                     bias=cols_in[:, 1:2]).then_inc(q_cp, 1)

            def copy_v(half):
                act.wait_ge(v_mm, half + 1)
                nc.scalar.activation(v_all[:, 2 * half:2 * half + 2, :, :],
                                     ps_uv[0][:, :].rearrange("t (p b h) -> t p b h", p=2, b=2), ACT.Copy)\
                    .then_inc(v_cp, 1)

            def first_part(p):
                act.wait_ge(q_cp, p // 2 + 1)
                act.wait_ge(k_cp, p // 2 + 1)
                nc.scalar.activation(qk_parts[:, p, 0, :, :], qk_all[:, p, :, :], ACT.Copy).then_inc(part_cp[0], 1)

            def second_part(p):
                act.wait_ge(rest_done, p)
                nc.scalar.activation(qk_parts[:, p, 1, :, :], qk_rest[:, :, :], ACT.Copy).then_inc(part_cp[1], 1)

            def round_w12(q):
                if q == 0:
                    act.wait_ge(in_w12[0], 16)
                    act.wait_ge(in_w12[1], 16)
                nc.scalar.activation(w12_hi[:, :, 2 * q:2 * q + 2, :], w12_nat[:, :, 2 * q:2 * q + 2, :], ACT.Copy)\
                    .then_inc(hi_done, 1)

            act.dma_start(proj_w[:, 2, :], wo).then_inc(in_wo, 16)
            act.wait_ge(c_id, 2)
            nc.scalar.activation(ident_b[:, :], ident[:, :], ACT.Copy).then_inc(c_id, 1)
            act.wait_ge(in_cols, 48)
            copy_q(0)
            first_part(1)
            copy_v(0)
            second_part(1)
            for g in range(GROUPS):
                exps(0, g)
                if g == 1:
                    copy_second_xT()
                if g == 2:
                    round_w12(0)
                if g == 3:
                    round_w12(1)
                if g == 4:
                    copy_q(1)
                    round_w12(2)
                if g == 5:
                    first_part(2)
                if g == 6:
                    second_part(2)
                if g == 7:
                    first_part(3)
            exps(1, 0)
            exps(1, 1)
            copy_probsT(1, 0)
            exps(1, 2)
            copy_probsT(1, 1)
            copy_v(1)
            copy_probsT(1, 2)
            exps(1, 3)
            second_part(3)
            copy_probsT(1, 3)

            def body(f, ahead):
                for s in range(SLOTS):
                    if s == 15:
                        copy_duT(f + 1)
                    tanh_slot(f, s)
                    if s == 8:
                        copy_invT(f + 1)
                    if s == 1:
                        tanh_gap(f)
                    if group_at(f, s - 1, ahead):
                        exps(*group_at(f, s - 1, ahead))
                    if group_at(f, s - 2, ahead):
                        copy_probsT(*group_at(f, s - 2, ahead))

            with act.Fori(0, PAIRS - 2) as f:
                body(f, True)
            body(PAIRS - 2, False)
            for s in range(SLOTS):
                tanh_slot(PAIRS - 1, s)
                if s == 1:
                    tanh_gap(PAIRS - 1)

        @block.vector
        def _(dve):
            def row_max(p, g):
                dve.wait_ge(s_done, GROUPS * p + g + 1)
                nc.vector.tensor_reduce(neg_max[:, g % 2, :], ps_s[g % 2][:, :].rearrange("i (c j) -> i c j", c=QC),
                                        AX, ALU.max, negate=True).then_inc(max_done, 1)

            def copy_probsT(p, g):
                G = GROUPS * p + g
                dve.wait_ge(pT_done, G + 1)
                if g >= 2 or later(p):
                    dve.wait_ge(av_done, G - 1)
                nc.vector.tensor_copy(probsT[:, g % 2, :, :], ps_t[:, :].rearrange("j (c i) -> j c i", c=QC))\
                    .then_inc(pT_cp, 1)

            def stage_first_values():
                dve.wait_ge(c_zero, 1)
                dve.wait_ge(v_cp, 1)
                nc.vector.tensor_copy(
                    v_pad[:, :, :].rearrange("j n (r x) -> j n r x", r=QR)[:, :, :, 0:DH],
                    v_all[:, 0, :, :].rearrange("j b (c r d) -> j (b c) r d", c=QC, r=QR)).then_inc(v_staged, 2)

            def mask_keys(r):
                for c in range(QC):
                    h = QR * c + r
                    last = nc.vector.tensor_scalar(k_head[:, :, r, c, :],
                                                   qk_all[:, 0, 1, :].rearrange("k (b t) -> k b t", b=2),
                                                   head_rows[:, h:h + 1], None, ALU.mult)
                last.then_inc(k_masked, 1)

            def invert_sums(p, b):
                dve.wait_ge(exp_done, GROUPS * p + QR * (b + 1))
                nc.vector.reciprocal(inv_sum[:, b, :], row_sum[:, b, :, :].rearrange("i c r -> i (c r)"))\
                    .then_inc(inv_done, 1)
                if later(p):
                    dve.wait_ge(invT_mm, p)
                dve.wait_ge(inv_done, 2 * p + b + 1)
                nc.vector.tensor_copy(inv_rep[:, b, :].rearrange("i (h d) -> i h d", d=DH),
                                      inv_sum[:, b, :].rearrange("i (h a) -> i h a", a=1)
                                      .to_broadcast([T, H, DH])).then_inc(inv_spread, 1)

            def copy_invT(p):
                dve.wait_ge(invT_mm, p + 1)
                nc.vector.tensor_copy(invT[:, :, :], tail_bank(p, 8).rearrange("h (b i) -> h b i", b=2))\
                    .then_inc(invT_cp, 1)

            def norm_y(p):
                dve.wait_ge(av_done, GROUPS * p + GROUPS)
                dve.wait_ge(invT_cp, p + 1)
                nc.vector.tensor_tensor(yT[:, :, :], ps_m[:, 0:2 * T].rearrange("h (b i) -> h b i", b=2),
                                        invT[:, :, :], ALU.mult).then_inc(yT_cp, 1)

            def copy_duT(p):
                dve.wait_ge(duT_mm, p + 1)
                nc.vector.tensor_copy(duT[:, :, :], tail_bank(p, 14).rearrange("d (b s) -> d b s", b=2))\
                    .then_inc(duT_cp, 1)

            def first_residual(p):
                dve.wait_ge(o_done, p + 1)
                nc.vector.tensor_tensor(x1[:, :, 1:D + 1], tail_bank(p, 11).rearrange("t (b d) -> t b d", b=2),
                                        xbo_all[:, bass.ds(p, 1), :, :].rearrange("t p b d -> t (p b) d"),
                                        ALU.add).then_inc(x1_done, 1)
                if later(p):
                    dve.wait_ge(react_done, p)
                nc.vector.tensor_copy(coef_p[:, :, :], coef[:, bass.ds(p, 1), :, :]
                                      .rearrange("t p k b -> t (p k) b")).then_inc(coef_staged, 1)
                dve.wait_ge(x1_done, p + 1)
                nc.vector.tensor_copy(x1[:, :, 0:D + 2:D + 1], x1[:, :, 2:D:D - 3]).then_inc(x1_edges, 1)

            def react_first_pair():
                dve.wait_ge(coef_staged, 1)
                for b in range(2):
                    last = nc.vector.tensor_scalar(react[:, b, :], x1[:, b, 1:D + 1], coef_p[:, 2, b:b + 1],
                                                   coef_p[:, 3, b:b + 1], ALU.mult, ALU.add)
                last.then_inc(react_done, 1)
                dve.wait_ge(react_done, 1)
                nc.vector.tensor_tensor(react_x[:, :, :], react[:, :, :], x1[:, :, 1:D + 1], ALU.mult)\
                    .then_inc(rx_done, 1)

            def diffuse_channels(p):
                dve.wait_ge(side_done, p + 1)
                dve.wait_ge(rx_done, p + 1)
                for b in range(2):
                    nc.vector.scalar_tensor_tensor(du_part[:, b, :], side_sum[:, b, :], coef_p[:, 0, b:b + 1],
                                                   react_x[:, b, :], ALU.mult, ALU.add).then_inc(dup_done, 1)

            def diffuse_tokens(p):
                dve.wait_ge(lap_done, p + 1)
                for b in range(2):
                    dve.wait_ge(dup_done, 2 * p + b + 1)
                    last = nc.vector.scalar_tensor_tensor(du[:, b, :], tail_bank(p, 13)[:, D * b:D * b + D],
                                                          coef_p[:, 1, b:b + 1], du_part[:, b, :],
                                                          ALU.mult, ALU.add)
                last.then_inc(du_done, 1)

            def split_duT(p):
                if later(p):
                    dve.wait_ge(uv_done, SLOTS * p)
                dve.wait_ge(duT_cp, p + 1)
                flat = duT[:, :, :].rearrange("d b t -> d (b t)")
                nc.vector.tensor_copy(duT_hi[:, :], flat).then_inc(duh_cp, 1)
                dve.wait_ge(duh_cp, p + 1)
                nc.vector.tensor_tensor(duT_lo[:, :], flat, duT_hi[:, :].bitcast(F32), ALU.subtract)\
                    .then_inc(dul_cp, 1)

            def rank_experts(f):
                dve.wait_ge(lg_mm, f + 1)
                nc.vector.tensor_copy(logits[:, :, :], tail_bank(f, 15)[:, 0:2 * E].rearrange("t (b e) -> t b e", b=2))
                for b in range(2):
                    last = nc.vector.max(top8[:, b, :], tail_bank(f, 15)[:, E * b:E * b + E])
                last.then_inc(top_done, 1)

            def index_experts(f):
                dve.wait_ge(top_done, f + 1)
                nc.vector.tensor_tensor(gap[:, :].rearrange("t (b a) -> t b a", a=1), top8[:, :, 0:1],
                                        top8[:, :, 1:2], ALU.subtract).then_inc(gap_done, 1)
                for b in range(2):
                    last = nc.vector.max_index(top_i[:, b, :], top8[:, b, :], logits[:, b, :])
                last.then_inc(index_done, 1)
                dve.wait_ge(index_done, f + 1)
                nc.vector.tensor_copy(top_f[:, :, :], top_i[:, :, 0:2]).then_inc(index_f, 1)

            def weigh_experts(f):
                dve.wait_ge(index_f, f + 1)
                nc.vector.tensor_tensor(same[:, :, :], expert_f[:, :, :],
                                        top_f[:, :, :].rearrange("t b (k a) -> t (b k) a", a=1)
                                        .to_broadcast([T, 4, E]), ALU.is_equal).then_inc(compared, 1)
                dve.wait_ge(gap_tanh, f + 1)
                for k, sign in enumerate((0.25, -0.25)):
                    nc.vector.tensor_scalar(gate2[:, :, k:k + 1], gap_t[:, :].rearrange("t (b a) -> t b a", a=1),
                                            sign, 0.25, ALU.mult, ALU.add).then_inc(gate2_done, 1)

            def silu(f, s):
                dve.wait_ge(tanh_done, SLOTS * f + s + 1)
                if roomy(f, s):
                    dve.wait_ge(hid_done, SLOTS * f + s - 2)
                nc.vector.scalar_tensor_tensor(silu_of(f, s), tanh_u[:, s % 2, :], 1.0,
                                               uv_bank(f, s)[:, 0:2 * T], ALU.add, ALU.mult).then_inc(silu_done, 1)

            def gate_hidden(f, s):
                dve.wait_ge(silu_done, SLOTS * f + s + 1)
                if roomy(f, s):
                    dve.wait_ge(y_done, SLOTS * f + s - 3)
                nc.vector.tensor_tensor(hidden_of(f, s).rearrange("h b t -> h (b t)"), silu_of(f, s),
                                        uv_bank(f, s)[:, 2 * T:4 * T], ALU.mult).then_inc(hid_done, 1)

            def add_expert(f, e):
                dve.wait_ge(y_done, SLOTS * f + 2 * e + 2)
                if e == 0:
                    dve.wait_ge(gates_done, f + 1)
                else:
                    dve.wait_ge(acc_done, E * f + e)
                if e == E - 1:
                    dve.wait_ge(out_done, 16 * f + 1)
                for b in range(2):
                    base = x1[:, b, 1:D + 1] if e == 0 else acc[:, b, :]
                    into = result[:, b, :] if e == E - 1 else acc[:, b, :]
                    last = nc.vector.scalar_tensor_tensor(into, ps_y[e % 2][:, D * b:D * b + D],
                                                          gates[:, b, e:e + 1], base, ALU.mult, ALU.add)
                last.then_inc(acc_done, 1)

            def bias_h(half):
                dve.wait_ge(hT_mm, half + 1)
                part = slice(HALF * half, HALF * half + HALF)
                nc.vector.tensor_tensor(hT[:, part, :], ps_uv[1][:, :].rearrange("d (b t) -> d b t", b=HALF),
                                        cond_bias[:, part].rearrange("d (b a) -> d b a", a=1)
                                        .to_broadcast([D, HALF, T]), ALU.add).then_inc(hT_cp, 1)

            def bias_k(half):
                dve.wait_ge(k_mm, half + 1)
                nc.vector.tensor_scalar(qk_all[:, 2 * half:2 * half + 2, 1, :],
                                        k_bank(half)[:, :].rearrange("h (p t) -> h p t", p=2), bk_fold[:, 0:1], None,
                                        ALU.add).then_inc(k_cp, 1)

            def round_w12(q):
                dve.wait_ge(hi_done, q)
                nc.vector.tensor_copy(w12_hi[:, :, 2 * q:2 * q + 2, :], w12_nat[:, :, 2 * q:2 * q + 2, :])\
                    .then_inc(hi_done, 1)

            def w1_rest(q):
                dve.wait_ge(hi_done, q + 1)
                nc.vector.tensor_tensor(w12_lo[:, 0, 2 * q:2 * q + 2, :], w12_nat[:, 0, 2 * q:2 * q + 2, :],
                                        w12_hi[:, 0, 2 * q:2 * q + 2, :].bitcast(F32), ALU.subtract)\
                    .then_inc(lo_done, 1)

            nc.vector.memset(v_pad[:, :, :], 0.0).then_inc(c_zero, 1)
            nc.vector.memset(result[:, :, :], 0.0).then_inc(out_done, 1)
            dve.wait_ge(in_cond_b, 32)
            dve.wait_ge(c_iota, 2)
            nc.vector.tensor_copy(cat_f[:, :], cat_i[:, :]).then_inc(cast_done, 1)
            nc.vector.tensor_copy(part_f[:, :], part_i[:, :]).then_inc(cast_done, 1)
            nc.vector.tensor_copy(expert_f[:, :, :], expert_i[:, :, :]).then_inc(cast_done, 1)
            dve.wait_ge(cast_done, 3)
            nc.vector.tensor_scalar(onehot[:, :], cat_f[:, :], part_f[:, 0:1], None, ALU.is_equal)\
                .then_inc(onehot_done, 1)
            dve.wait_ge(lsr_tr, 1)
            nc.vector.tensor_copy(lsrT[:, :, :], ps_s[1][0:RANK, 0:256].rearrange("r (i h) -> r i h", i=2))\
                .then_inc(lsr_cp, 1)
            dve.wait_ge(xT_mm, 1)
            nc.vector.tensor_copy(xT[:, :, :], ps_uv[0][:, :].rearrange("d (b t) -> d b t", b=HALF)).then_inc(xT_cp, 1)
            dve.wait_ge(proj_tr, 1)
            nc.vector.tensor_copy(proj_wT[:, 0:2, :], ps_s[0][:, 0:256].rearrange("d (i h) -> d i h", i=2))\
                .then_inc(proj_cp, 1)
            dve.wait_ge(fold_mm, 1)
            dve.wait_ge(c_heads, 3)
            nc.vector.scalar_tensor_tensor(
                fold[:, :].rearrange("k (h d) -> k h d", h=H), ps_t[:, 0:128].rearrange("k (h d) -> k h d", h=H), SCALE,
                head_rows[:, :].rearrange("k (h a) -> k h a", a=1).to_broadcast([128, H, DH]), ALU.mult, ALU.mult)\
                .then_inc(fold_cp, 1)
            dve.wait_ge(cb_mm, 1)
            nc.vector.tensor_copy(cond_bias[:, :], ps_y[0][:, 0:B]).then_inc(cb_cp, 1)
            dve.wait_ge(cb_cp, 1)
            bias_h(0)
            dve.wait_ge(wk_mm, 1)
            nc.vector.tensor_copy(wkT[:, :], ps_y[1][:, 0:128]).then_inc(wk_cp, 1)
            nc.vector.tensor_copy(bk_fold[:, :], ps_y[1][:, 128:129]).then_inc(wk_cp, 1)
            dve.wait_ge(wk_cp, 2)
            bias_k(0)
            dve.wait_ge(k_cp, 1)
            mask_keys(0)
            mask_keys(1)
            dve.wait_ge(wo_tr, 1)
            nc.vector.tensor_copy(proj_wT[:, 2, :], ps_m[:, 0:128]).then_inc(wo_cp, 1)

            def add_bias():
                dve.wait_ge(bv_mm, 1)
                dve.wait_ge(in_rows, 16)
                nc.vector.tensor_tensor(bo_rows[:, :], bo_rows[:, :], ps_m[:, 128:256], ALU.add).then_inc(bias_done, 1)

            def prepare_coefficients():
                def rows(i):
                    return coef_rows[:, i, :].rearrange("t (p b) -> t p b", b=2)

                dve.wait_ge(in_coef, 48)
                nc.vector.tensor_copy(coef[:, :, 0, :], rows(0)).then_inc(coef_done, 1)
                nc.vector.tensor_copy(coef[:, :, 1, :], rows(1)).then_inc(coef_done, 1)
                nc.vector.tensor_scalar(coef[:, :, 2, :], rows(2), -1.0, None, ALU.mult).then_inc(coef_done, 1)
                nc.vector.scalar_tensor_tensor(coef[:, :, 3, :], rows(0), -2.0, rows(2), ALU.mult, ALU.add)\
                    .then_inc(coef_done, 1)

            for g in range(GROUPS):
                row_max(0, g)
                if g >= 2:
                    copy_probsT(0, g - 2)
                if g == QR:
                    invert_sums(0, 0)
                if g == 0:
                    mask_keys(2)
                if g == 1:
                    mask_keys(3)
                    stage_first_values()
                    add_bias()
                if g == 2:
                    prepare_coefficients()
                if g == 3:
                    bias_h(1)
                if g == 4:
                    w1_rest(0)
                if g == 5:
                    bias_k(1)
                    w1_rest(1)
                if g == 6:
                    round_w12(3)
                if g == 7:
                    w1_rest(2)
            copy_probsT(0, GROUPS - 2)
            row_max(1, 0)
            invert_sums(0, 1)
            copy_probsT(0, GROUPS - 1)
            copy_invT(0)
            row_max(1, 1)
            norm_y(0)
            w1_rest(3)
            dve.wait_ge(xbo_done, 2)
            dve.wait_ge(coef_done, 4)
            first_residual(0)
            row_max(1, 2)
            react_first_pair()
            diffuse_channels(0)
            diffuse_tokens(0)
            row_max(1, 3)
            copy_duT(0)
            split_duT(0)
            invert_sums(1, 0)
            row_max(1, 4)

            def body(f, ahead):
                for s in range(SLOTS):
                    if s >= 3 and s % 2 == 1 and not roomy(f, s):
                        add_expert(f, (s - 3) // 2)
                    if s >= 13 and s % 2 == 1 and roomy(f, s):
                        add_expert(f, (s - 5) // 2)
                    if s >= 2 and s % 2 == 0 and group_at(f, s - 1, ahead):
                        row_max(*group_at(f, s - 1, ahead))
                    early = 0 if ahead else 1
                    if s == 12 - early:
                        first_residual(f + 1)
                    if s == 13 and not ahead:
                        diffuse_channels(f + 1)
                    if s == 14 - early:
                        diffuse_tokens(f + 1)
                    if s == SLOTS - 1 and not ahead:
                        split_duT(f + 1)
                    if s == 0:
                        rank_experts(f)
                    silu(f, s)
                    if s == 9 and not ahead:
                        norm_y(f + 1)
                    if not roomy(f, s):
                        gate_hidden(f, s)
                    elif roomy(f, s - 1):
                        gate_hidden(f, s - 1)
                    if s == SLOTS - 1 and ahead:
                        split_duT(f + 1)
                    if s == 7:
                        invert_sums(f + 1, 1)
                    if s == 9 and ahead:
                        norm_y(f + 1)
                    if s == 13 and ahead:
                        diffuse_channels(f + 1)
                    if s == 0:
                        index_experts(f)
                    if s == 1:
                        weigh_experts(f)
                if ahead:
                    invert_sums(f + 2, 0)
                    row_max(f + 2, QR)
                    add_expert(f, E - 1)

            with dve.Fori(0, PAIRS - 2) as f:
                body(f, True)
            body(PAIRS - 2, False)
            rank_experts(PAIRS - 1)
            for n in range(SLOTS * (PAIRS - 1), SLOTS * PAIRS + 1):
                if n < SLOTS * PAIRS:
                    silu(n // SLOTS, n % SLOTS)
                gate_hidden((n - 1) // SLOTS, (n - 1) % SLOTS)
                if n == SLOTS * (PAIRS - 1):
                    index_experts(PAIRS - 1)
                if n == SLOTS * (PAIRS - 1) + 1:
                    weigh_experts(PAIRS - 1)
                if n % 2 == 1:
                    add_expert((n - 5) // SLOTS, (n - 5) % SLOTS // 2)
            for e in range(E - 2, E):
                add_expert(PAIRS - 1, e)

        @block.tensor
        def _(pe):
            mm = nc.tensor.matmul

            def transpose_x(half):
                pe.wait_ge(in_x[half], 16)
                if half:
                    pe.wait_ge(v_cp, half)
                for b in range(HALF):
                    last = nc.tensor.transpose(ps_uv[0][:, T * b:T * b + T], x_nat[:, HALF * half + b, :], ident[:, :])
                last.then_inc(xT_mm, 1)

            def condition(half):
                pe.wait_ge(xT_cp, half + 1)
                if half:
                    pe.wait_ge(hT_cp, half)
                for b in range(HALF):
                    pe.wait_ge(in_cond_w[HALF * half + b], 16)
                    last = mm(ps_uv[1][:, T * b:T * b + T], cond_w_sb[:, HALF * half + b, :],
                              xT[:, b, :], start=True, stop=True)
                last.then_inc(hT_mm, 1)

            def project_q(half):
                pe.wait_ge(hT_cp, half + 1)
                if half:
                    pe.wait_ge(xT_cp, half + 1)
                mm(q_bank(half)[:, :], proj_wT[:, 0, :], hT[:, HALF * half:HALF * half + HALF, :],
                   start=True, stop=True).then_inc(q_mm, 1)

            def project_k(half):
                mm(k_bank(half)[:, :], wkT[:, :], hT[:, HALF * half:HALF * half + HALF, :],
                   start=True, stop=True).then_inc(k_mm, 1)

            def project_v(half):
                pe.wait_ge(q_cp if half else xT_cp, half + 1)
                for b in range(HALF):
                    last = mm(ps_uv[0][:, D * b:D * b + D], hT[:, HALF * half + b, :], proj_wT[:, 1, :],
                              start=True, stop=True)
                last.then_inc(v_mm, 1)

            def scores(p, g):
                G = GROUPS * p + g
                b, r = g // QR, g % QR
                first_pair = isinstance(p, int) and p == 0
                if first_pair:
                    pe.wait_ge(q_cp, 1)
                    pe.wait_ge(k_masked, r + 1)
                elif isinstance(p, int) and p == 1:
                    if g == 0:
                        pe.wait_ge(q_in[1], 16)
                        pe.wait_ge(k_in[1], 16)
                elif r == 0:
                    pe.wait_ge(stack_in[b], 16 * (p - 1))
                if g >= 2 or later(p):
                    pe.wait_ge(exp_done, G - 1)
                if later(p) and g == 5:
                    pe.wait_ge(top_done, p)
                elif g in (1, 3, 4) and not (isinstance(p, int) and p < 2):
                    pe.wait_ge({1: invT_cp, 3: x1_done, 4: duT_cp}[g], p)
                mm(ps_s[g % 2][:, :], ident_b[:, :], causal_b[:, :, :], start=True, stop=False, skip_group_check=True)
                if first_pair:
                    last = mm(ps_s[g % 2][:, :], qk_all[:, 0, 0, T * b:T * b + T], k_head[:, b, r, :, :],
                              start=False, stop=True, skip_group_check=True)
                else:
                    for c in range(QC):
                        h = QR * c + r
                        last = mm(ps_s[g % 2][:, T * c:T * c + T], stack[:, 0, h, T * b:T * b + T],
                                  stack[:, 1, h, T * b:T * b + T],
                                  start=False, stop=True, skip_group_check=True)
                last.then_inc(s_done, 1)

            def transpose_probs(p, g):
                G = GROUPS * p + g
                pe.wait_ge(exp_done, G + 1)
                if g >= 1 or later(p):
                    pe.wait_ge(pT_cp, G)
                for c in range(QC):
                    last = nc.tensor.transpose(ps_t[:, T * c:T * c + T], probs[:, g % 2, c, :], ident[:, :])
                last.then_inc(pT_done, 1)

            def weigh_values(p, g):
                b, r = g // QR, g % QR
                pe.wait_ge(pT_cp, GROUPS * p + g + 1)
                if r == 0:
                    pe.wait_ge(v_staged, 2 * p + b + 1)
                if g == 0 and later(p):
                    pe.wait_ge(yT_cp, p)
                for c in range(QC):
                    last = mm(ps_m[32 * c:32 * c + 32, T * b:T * b + T], v_pad[:, QC * b + c, 32 * r:32 * r + 32],
                              probsT[:, g % 2, c, :], start=r == 0, stop=r == QR - 1)
                last.then_inc(av_done, 1)

            def transpose_inverses(p):
                pe.wait_ge(inv_spread, 2 * p + 2)
                for b in range(2):
                    last = nc.tensor.transpose(tail_bank(p, 8)[:, T * b:T * b + T], inv_rep[:, b, :], ident[:, :])
                last.then_inc(invT_mm, 1)

            def project_out(p):
                pe.wait_ge(yT_cp, p + 1)
                for b in range(2):
                    last = mm(tail_bank(p, 11)[:, D * b:D * b + D], yT[:, b, :], proj_wT[:, 2, :], start=True, stop=True)
                last.then_inc(o_done, 1)

            def laplace_tokens(p):
                pe.wait_ge(x1_done, p + 1)
                mm(tail_bank(p, 13), stencil[:, :], x1[:, :, 1:D + 1], start=True, stop=True).then_inc(lap_done, 1)

            def transpose_du(p):
                pe.wait_ge(du_done, p + 1)
                for b in range(2):
                    last = nc.tensor.transpose(tail_bank(p, 14)[:, T * b:T * b + T], du[:, b, :], ident[:, :])
                last.then_inc(duT_mm, 1)

            def score_experts(p):
                pe.wait_ge(duT_cp, p + 1)
                for b in range(2):
                    last = mm(tail_bank(p, 15)[:, E * b:E * b + E], duT[:, b, :], w_gate_sb[:, :], start=True, stop=True)
                last.then_inc(lg_mm, 1)

            def expert_up(f, s):
                e, c = s // 2, s % 2
                if s == 0:
                    pe.wait_ge(dul_cp, f + 1)
                if s >= 2 or roomy(f, s):
                    pe.wait_ge(hid_done, SLOTS * f + s - (3 if roomy(f, s) else 1))
                for i in range(2):
                    w_hi = w12_hi[:, i, e, 128 * c:128 * c + 128]
                    w_lo = w12_lo[:, i, e, 128 * c:128 * c + 128]
                    into = uv_bank(f, s)[:, 2 * T * i:2 * T * i + 2 * T]
                    mm(into, w_hi, duT_hi[:, :], start=True, stop=False)
                    mm(into, w_hi, duT_lo[:, :], start=False, stop=False)
                    last = mm(into, w_lo, duT_hi[:, :], start=False, stop=True)
                last.then_inc(uv_done, 1)

            def expert_down(f, s):
                e, c = s // 2, s % 2
                pe.wait_ge(hid_done, SLOTS * f + s + 1)
                if c == 0 and (e >= 2 or roomy(f, s)):
                    pe.wait_ge(acc_done, E * f + e - 1)
                for b in range(2):
                    last = mm(ps_y[e % 2][:, D * b:D * b + D], hidden_of(f, s)[:, b, :], w3_sb[:, e, c, :],
                              start=c == 0 and b == 0, stop=c == 1, skip_group_check=True)
                last.then_inc(y_done, 1)

            def keep_busy(n):
                for _ in range(n):
                    nc.tensor.transpose(ps_m[:, 0:128], ident[:, :], ident[:, :])

            pe.wait_ge(c_id, 2)
            keep_busy(18)
            pe.wait_ge(in_lsr, 32)
            for i in range(2):
                last = nc.tensor.transpose(ps_s[1][0:RANK, 128 * i:128 * i + 128], lsr_nat[:, i, :], ident[:, :])
            last.then_inc(lsr_tr, 1)
            transpose_x(0)
            pe.wait_ge(lsr_cp, 1)
            mm(ps_t[:, 0:128], lsrT[:, 1, :], lsrT[:, 0, :], start=True, stop=True).then_inc(fold_mm, 1)
            pe.wait_ge(in_proj, 32)
            for i in range(2):
                last = nc.tensor.transpose(ps_s[0][:, 128 * i:128 * i + 128], proj_w[:, i, :], ident[:, :])
            last.then_inc(proj_tr, 1)
            pe.wait_ge(onehot_done, 1)
            mm(ps_y[0][:, 0:B], cond_b_sb[:, :], onehot[:, :], start=True, stop=True).then_inc(cb_mm, 1)
            keep_busy(2)
            condition(0)
            pe.wait_ge(fold_cp, 1)
            pe.wait_ge(in_wk, 16)
            pe.wait_ge(in_cols, 48)
            mm(ps_y[1][:, 0:128], wk_nat[:, :], fold[:, :], start=True, stop=True)
            mm(ps_y[1][:, 128:129], fold[:, :], cols_in[:, 0:1], start=True, stop=True).then_inc(wk_mm, 1)
            keep_busy(6)
            pe.wait_ge(wk_cp, 2)
            pe.wait_ge(hT_cp, 1)
            project_k(0)
            pe.wait_ge(proj_cp, 1)
            pe.wait_ge(cb_cp, 1)
            project_q(0)
            project_v(0)
            pe.wait_ge(in_wo, 16)
            nc.tensor.transpose(ps_m[:, 0:128], proj_w[:, 2, :], ident[:, :]).then_inc(wo_tr, 1)
            pe.wait_ge(c_id, 3)
            pe.wait_ge(c_causal, 2)
            for g in range(GROUPS + 1):
                scores(g // GROUPS, g % GROUPS)
                if g == 1:
                    pe.wait_ge(wo_cp, 1)
                    mm(ps_m[:, 128:256], cols_in[:, 2:3].to_broadcast([D, T]), proj_wT[:, 2, :],
                       start=True, stop=True).then_inc(bv_mm, 1)
                if 2 <= g <= 5:
                    (transpose_x, condition, project_q, project_k)[g - 2](1)
                if g >= 2:
                    transpose_probs(0, g - 2)
                if g == 3:
                    pe.wait_ge(bias_done, 1)
                if g >= 3:
                    weigh_values(0, g - 3)
            scores(1, 1)
            transpose_probs(0, GROUPS - 1)
            weigh_values(0, GROUPS - 2)
            transpose_inverses(0)
            weigh_values(0, GROUPS - 1)
            transpose_probs(1, 0)
            project_out(0)
            scores(1, 2)
            pe.wait_ge(c_stencil, 6)
            laplace_tokens(0)
            weigh_values(1, 0)
            transpose_probs(1, 1)
            scores(1, 3)
            project_v(1)
            weigh_values(1, 1)
            transpose_probs(1, 2)
            transpose_du(0)
            scores(1, 4)
            weigh_values(1, 2)
            transpose_probs(1, 3)
            pe.wait_ge(in_gate, 16)
            score_experts(0)
            pe.wait_ge(v_cp, 2)
            pe.wait_ge(lo_done, 2 * QC)
            pe.wait_ge(in_w3, 16)

            def body(f, ahead):
                for s in range(SLOTS):
                    expert_up(f, s)
                    if s == 8 and ahead:
                        transpose_inverses(f + 1)
                    if group_at(f, s, ahead) and s < SLOTS - 1:
                        scores(*group_at(f, s, ahead))
                    if s >= 1 and not roomy(f, s):
                        expert_down(f, s - 1)
                    if s >= 12 and roomy(f, s):
                        expert_down(f, s - 3)
                    if group_at(f, s - 2, ahead):
                        transpose_probs(*group_at(f, s - 2, ahead))
                    if group_at(f, s - 3, ahead):
                        weigh_values(*group_at(f, s - 3, ahead))
                    early = 0 if ahead else 1
                    if s == 8 and not ahead:
                        transpose_inverses(f + 1)
                    if s == 11 - early:
                        project_out(f + 1)
                    if s == 13 - early:
                        laplace_tokens(f + 1)
                    if s == 14:
                        transpose_du(f + 1)
                    if group_at(f, s, ahead) and s == SLOTS - 1:
                        scores(*group_at(f, s, ahead))
                    if s == SLOTS - 1:
                        score_experts(f + 1)
                if ahead:
                    expert_down(f, SLOTS - 1)

            with pe.Fori(0, PAIRS - 2) as f:
                body(f, True)
            body(PAIRS - 2, False)
            expert_down(PAIRS - 2, SLOTS - 3)
            expert_up(PAIRS - 1, 0)
            for n in range(SLOTS * (PAIRS - 1) + 1, SLOTS * PAIRS + 3):
                if n < SLOTS * PAIRS:
                    expert_up(n // SLOTS, n % SLOTS)
                expert_down((n - 3) // SLOTS, (n - 3) % SLOTS)


_INS = ["x", "itok_B_0_63", "condB_zX", "condB_zY", "condB_zR", "L0_cond_W", "L0_cond_b", "L0_attn_Wq", "L0_attn_bq",
        "L0_attn_Wk", "L0_attn_bk", "L0_attn_Wv", "L0_attn_bv", "L0_attn_Wo", "L0_attn_bo", "L0_attn_Wq_lsr",
        "L0_attn_Wk_lsr", "L0_ffn_Wg", "L0_ffn_W1", "L0_ffn_W2", "L0_ffn_W3"]
_OUT = ((8, 128, 128), "float32")


def kernel(**inputs):
    import numpy as _np
    import concourse.bacc as _bacc
    from concourse import mybir as _mybir
    from concourse.bass_utils import run_bass_kernel_spmd as _run

    nc = _bacc.Bacc("TRN2", target_bir_lowering=False, num_devices=1)
    arrays, args = {}, []
    for name in _INS:
        a = _np.ascontiguousarray(inputs[name])
        arrays[f"in_{name}_dram"] = a
        args.append(nc.dram_tensor(f"in_{name}_dram", a.shape, _mybir.dt.from_np(a.dtype), kind="ExternalInput").ap())
    shape, dtype = _OUT
    args.append(nc.dram_tensor("out_dram", shape, _mybir.dt.from_np(_np.dtype(dtype)), kind="ExternalOutput").ap())
    adaln_attention_reaction_moe(nc, *args)
    r = _run(nc, [arrays], core_ids=[0])
    return r.results[0]["out_dram"]
```
